# Optimizing a Trainium2 kernel written in Bass

```python
import numpy as np
import jax
import jax.numpy as jnp

def _softmax(x, axis=-1):
    return jax.nn.softmax(x, axis=axis)

def _gelu(x):
    return jax.nn.gelu(x, approximate=True)

def _silu(x):
    return jax.nn.silu(x)

def _sigmoid(x):
    return jax.nn.sigmoid(x)

def _layernorm(x, axis=-1, eps=1e-05):
    m = jnp.mean(x, axis=axis, keepdims=True)
    v = jnp.var(x, axis=axis, keepdims=True)
    return (x - m) / jnp.sqrt(v + eps)

def _scatter_add(tgt, idx, src, axis=0):
    return tgt.at[idx].add(src)

def _segment_sum(src, seg, n):
    return jax.ops.segment_sum(src, seg, n)
kernel_name = 'mk_gnn_preln_d1_gnn_r8_a41c92'

def setup_inputs(seed: int=0):
    np.random.seed(seed)
    _w = jnp.asarray

    def _rec_inputs():
        import jax
        import jax.numpy as jnp
        _gk = jax.random.key(seed)
        x = -0.0005121 + 1.001 * jax.random.normal(jax.random.fold_in(_gk, 1), (12500, 64), jnp.float32)
        src = jax.random.randint(jax.random.fold_in(_gk, 2), (200000,), 0, 12500, jnp.int32)
        dst = jnp.minimum((12500 * jax.random.uniform(jax.random.fold_in(_gk, 3), (200000,)) ** 2.0).astype(jnp.int32), 99999)
        _o = jnp.argsort(dst, stable=True)
        src = src[_o]
        dst = dst[_o]
        edge_type_64 = jax.random.randint(jax.random.fold_in(_gk, 12), (200000,), 0, 64, jnp.int32)
        edge_weight1 = jax.random.uniform(jax.random.fold_in(_gk, 13), (200000, 1), jnp.float32, 0.0, 0.999998)
        return (x, src, dst, edge_type_64, edge_weight1)
    x, src, dst, edge_type_64, edge_weight1 = _rec_inputs()

    def _L0_gnn_setup():
        import jax, jax.numpy as jnp
        import numpy as np
        N_NODES = 6250
        N_EDGES = 200000
        IN_F = 64
        OUT_F = 64
        NUM_RELS = 64
        NUM_BASES = 64
        BN_EPS = 1e-05
        key = jax.random.key(seed)
        ks = jax.random.split(key, 12)
        node_feats = jax.random.normal(ks[0], (N_NODES, IN_F), dtype=jnp.float32)
        src = jax.random.randint(ks[1], (N_EDGES,), 0, N_NODES, dtype=jnp.int32)
        dst = jax.random.randint(ks[2], (N_EDGES,), 0, N_NODES, dtype=jnp.int32)
        etype = jax.random.randint(ks[3], (N_EDGES,), 0, NUM_RELS, dtype=jnp.int32)
        norm = jax.random.uniform(ks[4], (N_EDGES, 1), dtype=jnp.float32)
        basis = jax.random.normal(ks[5], (NUM_BASES, IN_F, OUT_F), dtype=jnp.float32) * (1.0 / np.sqrt(IN_F))
        comp = jax.random.normal(ks[6], (NUM_RELS, NUM_BASES), dtype=jnp.float32) * (1.0 / np.sqrt(NUM_BASES))
        bias = jnp.zeros((OUT_F,), dtype=jnp.float32)
        res_w = jax.random.normal(ks[7], (OUT_F, IN_F), dtype=jnp.float32) * (1.0 / np.sqrt(IN_F))
        res_b = jnp.zeros((OUT_F,), dtype=jnp.float32)
        gamma = jnp.ones((OUT_F,), dtype=jnp.float32)
        beta = jnp.zeros((OUT_F,), dtype=jnp.float32)
        return {'node_feats': node_feats, 'src': src, 'dst': dst, 'etype': etype, 'norm': norm, 'basis': basis, 'comp': comp, 'bias': bias, 'res_w': res_w, 'res_b': res_b, 'gamma': gamma, 'beta': beta}
    _L0_gnn_all = _L0_gnn_setup()
    _L0_gnn_in = {k: v for k, v in _L0_gnn_all.items() if k in ('basis', 'comp', 'bias', 'res_w', 'res_b', 'gamma', 'beta')}
    del _L0_gnn_all
    return {'x': x, 'src': src, 'dst': dst, 'edge_type_64': edge_type_64, 'edge_weight1': edge_weight1, 'L0_gnn_basis': _L0_gnn_in['basis'], 'L0_gnn_comp': _L0_gnn_in['comp'], 'L0_gnn_bias': _L0_gnn_in['bias'], 'L0_gnn_res_w': _L0_gnn_in['res_w'], 'L0_gnn_res_b': _L0_gnn_in['res_b'], 'L0_gnn_gamma': _L0_gnn_in['gamma'], 'L0_gnn_beta': _L0_gnn_in['beta']}

def reference(x, src, dst, edge_type_64, edge_weight1, L0_gnn_basis, L0_gnn_comp, L0_gnn_bias, L0_gnn_res_w, L0_gnn_res_b, L0_gnn_gamma, L0_gnn_beta):
    import jax
    import jax.numpy as jnp

    def _L0_gnn_ref(node_feats, src, dst, etype, norm, basis, comp, bias, res_w, res_b, gamma, beta):
        import jax, jax.numpy as jnp
        import numpy as np
        N_NODES = 6250
        N_EDGES = 200000
        IN_F = 64
        OUT_F = 64
        NUM_RELS = 64
        NUM_BASES = 64
        BN_EPS = 1e-05
        N = node_feats.shape[0]
        R = comp.shape[0]
        W = jnp.einsum('rb,bio->rio', comp, basis)
        msg = node_feats[src] * norm
        seg = etype.astype(jnp.int32) * N + dst
        s = jax.ops.segment_sum(msg, seg, num_segments=R * N)
        s = s.reshape(R, N, -1)
        h = jnp.einsum('rni,rio->no', s, W) + bias
        h = jax.nn.relu(h)
        res = jax.nn.relu(node_feats @ res_w.T + res_b)
        y = h + res
        mean = jnp.mean(y, axis=0)
        var = jnp.var(y, axis=0)
        return (y - mean) * jax.lax.rsqrt(var + BN_EPS) * gamma + beta
    h = jnp.maximum(_layernorm(x, axis=-1), 0.0)
    x = x + _L0_gnn_ref(h, src, dst, edge_type_64, edge_weight1, L0_gnn_basis, L0_gnn_comp, L0_gnn_bias, L0_gnn_res_w, L0_gnn_res_b, L0_gnn_gamma, L0_gnn_beta)
    return x

_drawn_inputs = setup_inputs


def setup_inputs(seed=0):
    import zlib

    import numpy as np

    out = dict(_drawn_inputs(seed))
    spreads = {'L0_gnn_bias': (0.0, 0.278),
     'L0_gnn_res_b': (0.0, 0.1),
     'L0_gnn_gamma': (1.0, 0.2),
     'L0_gnn_beta': (0.0, 0.1)}
    factors = {}
    for name, (base, spread) in spreads.items():
        noise = np.random.default_rng([zlib.crc32(name.encode()), seed]).standard_normal(out[name].shape)
        drawn = base * np.exp(spread * noise) if base else spread * noise
        out[name] = jnp.asarray(drawn.astype(out[name].dtype))
    for name, factor in factors.items():
        out[name] = (out[name] * factor).astype(out[name].dtype)
    return out
```

```python
import math
from contextlib import ExitStack

import concourse.bass as bass
from concourse import mybir

F32 = mybir.dt.float32
I32 = mybir.dt.int32
ALU = mybir.AluOpType
ACT = mybir.ActivationFunctionType
AX = mybir.AxisListType.X

P = 128
BANK = 512
LN_EPS = 1e-5
BN_EPS = 1e-5
GT = 8
GE = GT * P
WIN = 192
CLS = 8
NZB = 4
ZT = 4
NZS = 4
NY = 16
NOH = 8
LNT = 14


def rgcn_kernel(nc, x, src, dst, etype, weight, basis, comp, bias, res_w, res_b, gamma, beta, out):
    N, F = x.shape
    E = src.shape[0]
    R = comp.shape[0]
    NT = math.ceil(N / P)
    LAST = N - (NT - 1) * P
    NQ = NT // 2
    NCLS = R // CLS
    NG = math.ceil(E / GE)
    LE = E - (NG - 1) * GE
    NTILES = math.ceil(E / P)
    GA, GB = P, NG - P
    NLN = NT // LNT
    assert NT % 2 == 0 and NT % LNT == 0 and CLS * F == BANK and 64 < GB <= P and F == 64 and R == 64
    DUMP = NT * P
    ROWS = DUMP + P

    table = nc.dram_tensor("z_table", [NCLS * N * CLS, F], F32)
    accd = nc.dram_tensor("acc_rows", [ROWS, F], F32)

    with ExitStack() as ctx:
        def sb(name, shape, dt=F32):
            return ctx.enter_context(nc.sbuf_tensor(name, shape, dt))

        def sem(name):
            return ctx.enter_context(nc.semaphore(name))

        ARENA = NT * P + WIN + 16
        acc = sb("acc", [P, ARENA])
        ar_f = acc[:, 0:6 * 2 * GE].rearrange("p (a c n) -> p a c n", a=6, c=2)
        ar_i = acc[:, 0:6 * 2 * GE].bitcast(I32).rearrange("p (a c n) -> p a c n", a=6, c=2)
        dst_i, src_i, ety_i, cls_i = (ar_i[:, k] for k in range(4))
        idx_f, ety_f = ar_f[:, 1], ar_f[:, 2]
        rel_f, wgt_f = ar_f[:, 4], ar_f[:, 5]
        xs = sb("xs", [P, NT, F])
        xnT = sb("xnT", [P, NQ, P])
        basis_sb = xnT[0:R, 0:F * F // P, :].rearrange("b q n -> b (q n)").rearrange("b (i o) -> b i o", o=F)
        w_sb = sb("w_sb", [P, R, F])
        zst = sb("zst", [P, NZS, ZT, BANK])
        zflat = zst[:, :, :, :].rearrange("p s t n -> p (s t n)")
        xr = zflat[:, 0:NT * F].rearrange("p (t f) -> p t f", f=F)
        sq = sb("sq", [P, 2, LNT, F])
        mom = sb("mom", [P, 4, NT])
        idx_all = sb("idx_all", [P, NG * GT], I32)
        rel_all = sb("rel_all", [P, NG * GT])
        wgt_all = sb("wgt_all", [P, NG * GT])
        oh = sb("oh", [P, NOH, WIN])
        ys = sb("ys", [P, NY, F])
        ident = sb("ident", [P, P])
        stack2 = sb("stack2", [P, F])
        ones = sb("ones", [P, P])
        lower = sb("lower", [P, P])
        iota = sb("iota", [P, WIN])
        dumprow = sb("dumprow", [P, 1])
        comp_sb = sb("comp_sb", [R, R])
        compT = sb("compT", [R, R])
        resw_sb = sb("resw_sb", [F, 2 * F])
        reswT = sb("reswT", [P, F])
        cols = sb("cols", [F, 4])
        gstat = sb("gstat", [P, 2, 3])
        base_i = sb("base_i", [1, NG], I32)
        span_r = sb("span_r", [1, NG])
        flag_f = sb("flag_f", [1, 2])
        flag_i = sb("flag_i", [1, 1], I32)
        res_t = sb("res_t", [F, 2, BANK])
        BC = 25
        bst = sb("bst", [F, BC, 6])
        bmv = sb("bmv", [F, 8])
        diag = sb("diag", [F + 1, F])
        gdst = sb("gdst", [P, 2])
        gdstb = sb("gdstb", [P, P])
        geq = sb("geq", [P, P])
        gjunk = sb("gjunk", [P, P])
        gnum = sb("gnum", [P, 4])
        gidx = sb("gidx", [P, 1], I32)
        gsidx = sb("gsidx", [P, 1], I32)
        gy = sb("gy", [P, F])
        gyn = sb("gyn", [P, F])
        gsum = sb("gsum", [P, F])

        zps = ctx.enter_context(nc.psum_tensor("zps", [P, NZB, BANK], F32))
        aps = ctx.enter_context(nc.psum_tensor("aps", [P, 2, BANK], F32))
        mps = ctx.enter_context(nc.psum_tensor("mps", [P, 2, BANK], F32))
        mflat = mps[:, :, :].rearrange("p b n -> p (b n)")

        s_x = [sem(f"s_x{c}") for c in range(NLN)]
        s_small, s_basis = sem("s_small"), sem("s_basis")
        s_dst, s_idx, s_wgt = sem("s_dst"), sem("s_idx"), sem("s_wgt")
        s_pad = sem("s_pad")
        s_cst, s_pc = sem("s_cst"), sem("s_pc")
        s_xc, s_sq, s_var, s_dev, s_ln = (sem(n) for n in ("s_xc", "s_sq", "s_var", "s_dev", "s_ln"))
        s_pz, s_ez = sem("s_pz"), sem("s_ez")
        s_zst = [sem(f"s_zst{k}") for k in range(NZS)]
        s_met, s_mt, s_me = sem("s_met"), sem("s_mt"), sem("s_me")
        s_flag = sem("s_flag")
        s_y = [sem(f"s_y{k}") for k in range(NY)]
        s_oh, s_agg, s_acc = sem("s_oh"), sem("s_agg"), sem("s_acc")
        s_dv = sem("s_dv")
        s_sum = sem("s_sum")
        s_g = {k: sem(f"s_g_{k}") for k in
               ("dst", "mt", "me", "zero", "clr", "bcast", "row", "idx", "y", "mul", "mm", "sum", "add", "back", "tp", "tc", "go")}
        s_e1, s_er, s_eh, s_ey = sem("s_e1"), sem("s_er"), sem("s_eh"), sem("s_ey")
        s_diag, s_sh, s_shc, s_o, s_oc, s_out = (sem(n) for n in ("s_diag", "s_sh", "s_shc", "s_o", "s_oc", "s_out"))

        J_W = 2
        J_X = J_W + F // CLS
        NXJ = math.ceil(NQ / 4)
        J_Z = J_X + NXJ
        ZG = [(t, min(ZT, NT - 1 - t)) for t in range(0, NT - 1, ZT)] + [(NT - 1, 1)]
        STORES = [(c, t0, k) for c in range(NCLS) for t0, k in ZG]
        zview = table[:, :].rearrange("(c n r) f -> c n (r f)", c=NCLS, r=CLS)
        ECH = [(c, min(BANK, N - c)) for c in range(0, N, BANK)]

        def evac_done_of_store(n):
            return J_Z + sum(k for _, _, k in STORES[:n + 1])

        def fast_path_flag(e):
            e.wait_ge(s_flag, 1)
            return e.value_load(flag_i[0:1, 0:1], min_val=0, max_val=1)

        block = ctx.enter_context(nc.Block())

        @block.sync
        def _(e):
            xv = x[0:(NT - 1) * P, :].rearrange("(t p) f -> p t f", p=P)
            for c in range(NLN):
                t0, t1 = c * LNT, min((c + 1) * LNT, NT - 1)
                e.dma_start(xs[:, t0:t1, :], xv[:, t0:t1, :]).then_inc(s_x[c], 16)
            e.wait_ge(s_pad, 1)
            e.dma_start(xs[0:LAST, NT - 1, :], x[(NT - 1) * P:N, :]).then_inc(s_x[NLN - 1], 16)
            for n, (c, t0, k) in enumerate(STORES):
                e.wait_ge(s_ez, evac_done_of_store(n))
                rows = LAST if t0 == NT - 1 else P
                e.dma_start(zview[c, t0 * P:t0 * P + (k - 1) * P + rows, :].rearrange("(t p) w -> p t w", p=rows),
                            zst[0:rows, n % NZS, 0:k, :]).then_inc(s_zst[n % NZS], 16)
            flag = fast_path_flag(e)
            with e.If(flag < 1):
                e.wait_ge(s_g["zero"], 1)
                av = accd[:, :].rearrange("(p t) f -> p (t f)", p=P)
                width = ROWS // P * F
                cuts = list(range(0, width, 2048)) + [width]
                for a, b in zip(cuts, cuts[1:]):
                    e.dma_start(av[:, a:b], zflat[:, 0:b - a]).then_inc(s_g["clr"], 16)
                e.wait_ge(s_g["add"], 16 * NTILES)
                e.wait_ge(s_g["clr"], 16 * (len(cuts) - 1))
                e.dma_start(xr, accd[0:NT * P, :].rearrange("(t p) f -> p t f", p=P)).then_inc(s_g["back"], 16)
            ov = out[0:(NT - 1) * P, :].rearrange("(t p) f -> p t f", p=P)
            for n, t0 in enumerate(range(0, NT, 8)):
                t1 = min(t0 + 8, NT - 1)
                e.wait_ge(s_oc, n + 1)
                e.dma_start(ov[:, t0:t1, :], xs[:, t0:t1, :]).then_inc(s_out, 16)
            e.dma_start(out[(NT - 1) * P:N, :], xs[0:LAST, NT - 1, :]).then_inc(s_out, 16)
            e.wait_ge(s_out, 16 * (math.ceil(NT / 8) + 1))

        @block.gpsimd
        def _(e):
            e.memset(ident[:, :], 0.0).then_inc(s_pc, 1)
            e.memset(stack2[:, :], 0.0).then_inc(s_pc, 1)
            e.memset(lower[:, :], 0.0).then_inc(s_pc, 1)
            e.memset(ones[:, :], 1.0)
            e.wait_ge(s_pc, 3)
            e.affine_select(out=ident[:, :], in_=ident[:, :], compare_op=ALU.not_equal, fill=1.0,
                            base=0, pattern=[[-1, P]], channel_multiplier=1).then_inc(s_cst, 1)
            e.affine_select(out=lower[:, :], in_=lower[:, :], compare_op=ALU.is_ge, fill=1.0,
                            base=0, pattern=[[1, P]], channel_multiplier=-1).then_inc(s_cst, 1)
            e.affine_select(out=stack2[:, :], in_=stack2[:, :], compare_op=ALU.not_equal, fill=1.0,
                            base=0, pattern=[[-1, F]], channel_multiplier=1).then_inc(s_pc, 1)
            e.wait_ge(s_pc, 4)
            e.affine_select(out=stack2[:, :], in_=stack2[:, :], compare_op=ALU.not_equal, fill=1.0,
                            base=-F, pattern=[[-1, F]], channel_multiplier=1).then_inc(s_cst, 1)
            e.iota(iota[:, :], [[1, WIN]], base=0, channel_multiplier=0,
                   allow_small_or_imprecise_dtypes=True).then_inc(s_cst, 1)
            e.iota(dumprow[:, :], [[1, 1]], base=DUMP, channel_multiplier=1,
                   allow_small_or_imprecise_dtypes=True).then_inc(s_cst, 1)
            for k in range(NZS):
                e.wait_ge(s_zst[k], 16 * len(range(k, len(STORES), NZS)))
            flag = fast_path_flag(e)
            with e.If(flag < 1):
                e.wait_ge(s_g["clr"], 16 * math.ceil(ROWS // P * F / 2048))
                with e.Fori(0, NTILES) as t:
                    e.tensor_copy(gidx[:, :], idx_all[:, bass.ds(t, 1)]).then_inc(s_g["idx"], 1)
                    e.wait_ge(s_g["idx"], t + 1)
                    e.sem_inc(s_g["go"], 1)
                    e.indirect_dma_start(out=gy[:, :], out_offset=None, in_=table[:, :],
                                         in_offset=bass.IndirectOffsetOnAxis(ap=gidx[:, :], axis=0)).then_inc(s_g["y"], 16)
                    e.wait_ge(s_g["sum"], t + 1)
                    e.sem_inc(s_g["go"], 1)
                    e.indirect_dma_start(out=accd[:, :], out_offset=bass.IndirectOffsetOnAxis(ap=gsidx[:, :], axis=0),
                                         in_=gsum[:, :], in_offset=None, compute_op=ALU.add).then_inc(s_g["add"], 16)
                    e.wait_ge(s_g["add"], t * 16 + 16)
            with e.Else():
                for t in range(NTILES):
                    if t >= NY:
                        e.wait_ge(s_agg, t - NY + 1)
                    e.indirect_dma_start(out=ys[:, t % NY, :], out_offset=None, in_=table[:, :],
                                         in_offset=bass.IndirectOffsetOnAxis(ap=idx_all[:, t:t + 1], axis=0)
                                         ).then_inc(s_y[t % NY], 16)

        @block.scalar
        def _(e):
            e.dma_start(comp_sb[:, :], comp).then_inc(s_small, 16)
            e.dma_start(resw_sb[:, 0:F], res_w).then_inc(s_small, 16)
            e.dma_start(resw_sb[:, F:2 * F], res_w).then_inc(s_small, 16)
            e.dma_start(basis_sb, basis).then_inc(s_basis, 16)
            for k, v in enumerate((bias, res_b, gamma, beta)):
                e.dma_start(cols[:, k:k + 1], v.rearrange("(f a) -> f a", a=1)).then_inc(s_small, 16)
            e.wait_ge(s_pad, 2)
            for arr, to, s in ((dst, dst_i, s_dst), (src, src_i, s_idx), (etype, ety_i, s_idx), (weight, wgt_f, s_wgt)):
                e.dma_start(to[:, 0, :], arr[0:P * GE].rearrange("(g n) -> g n", n=GE)).then_inc(s, 16)
                e.dma_start(to[0:64, 1, :], arr[P * GE:(P + 64) * GE].rearrange("(g n) -> g n", n=GE)).then_inc(s, 16)
                e.dma_start(to[64:GB - 1, 1, :], arr[(P + 64) * GE:(NG - 1) * GE].rearrange("(g n) -> g n", n=GE)).then_inc(s, 16)
                e.dma_start(to[GB - 1:GB, 1, 0:LE], arr[E - LE:E].rearrange("(g n) -> g n", n=LE)).then_inc(s, 16)
                if arr is not weight:
                    e.dma_start(to[GB - 1:GB, 1, LE:GE], arr[E - (GE - LE):E].rearrange("(g n) -> g n", n=GE - LE)).then_inc(s, 16)

            def take(job, to, frm):
                e.wait_ge(s_pz, job + 1)
                e.activation(to, frm, ACT.Copy).then_inc(s_ez, 1)

            def square(c):
                e.wait_ge(s_xc, c + 1)
                if c >= 2:
                    e.wait_ge(s_var, c - 1)
                e.activation(sq[:, c % 2, :, :], xr[:, c * LNT:(c + 1) * LNT, :], ACT.Square).then_inc(s_sq, 1)

            def deviation(c):
                e.wait_ge(s_var, c + 1)
                e.activation(mom[:, 3, c * LNT:(c + 1) * LNT], mom[:, 2, c * LNT:(c + 1) * LNT], ACT.Sqrt).then_inc(s_dev, 1)

            take(0, compT[:, :], zps[0:R, 0, 0:R])
            take(1, reswT[:, :], zps[:, 1, 0:F])
            for n in range(F // CLS):
                if n < NLN:
                    square(n)
                if n >= 1:
                    deviation(n - 1)
                job = J_W + n
                take(job, w_sb[:, :, n * CLS:(n + 1) * CLS],
                     zps[:, job % NZB, :].rearrange("p (o r) -> p r o", r=R))
            for n in range(NXJ):
                job, q0, q1 = J_X + n, 4 * n, min(4 * n + 4, NQ)
                take(job, xnT[:, q0:q1, :].rearrange("p q n -> p (q n)"), zps[:, job % NZB, 0:(q1 - q0) * P])
            job = J_Z
            for n, (c, t0, k) in enumerate(STORES):
                rows = LAST if t0 == NT - 1 else P
                if n >= NZS:
                    e.wait_ge(s_zst[n % NZS], 16 * (n // NZS))
                for i in range(k):
                    take(job, zst[0:rows, n % NZS, i, :], zps[0:rows, job % NZB, :])
                    job += 1

            for n, (c0, w) in enumerate(ECH):
                e.wait_ge(s_e1, n + 1)
                e.activation(acc[0:F, c0:c0 + w], aps[0:F, n % 2, 0:w], ACT.Relu, bias=cols[:, 0:1]).then_inc(s_eh, 1)
                if n >= 2:
                    e.wait_ge(s_ey, n - 1)
                e.activation(res_t[:, n % 2, :].rearrange("p (q h n) -> p h q n", q=2, h=2),
                             zps[0:F, 2 * (n % 2):2 * (n % 2) + 2, 0:BANK // 2].rearrange("p h (q n) -> p h q n", q=2),
                             ACT.Relu, bias=cols[:, 1:2]).then_inc(s_er, 1)
            e.wait_ge(s_diag, 1)
            e.activation(bmv[:, 3:4], bmv[:, 2:3], ACT.Sqrt).then_inc(s_diag, 1)
            e.wait_ge(s_sh, 1)
            e.activation(diag[F:F + 1, :], mps[F:F + 1, 0, 0:F], ACT.Copy).then_inc(s_shc, 1)

        @block.vector
        def _(e):
            steps = [0]

            def link(ins):
                steps[0] += 1
                ins.then_inc(s_dv, 1)
                e.wait_ge(s_dv, steps[0])

            e.memset(xs[:, NT - 1, :], 0.0).then_inc(s_pad, 1)
            e.memset(wgt_f[64:GB, 1, :], 0.0).then_inc(s_pad, 1)
            def centre(c):
                t0, t1 = c * LNT, (c + 1) * LNT
                e.wait_ge(s_x[c], 32 if c == NLN - 1 else 16)
                link(e.tensor_reduce(mom[:, 0, t0:t1], xs[:, t0:t1, :], AX, ALU.add))
                link(e.tensor_scalar(mom[:, 1, t0:t1], mom[:, 0, t0:t1], 1.0 / F, None, ALU.mult))
                e.tensor_tensor(xr[:, t0:t1, :], xs[:, t0:t1, :],
                                mom[:, 1, t0:t1].unsqueeze(2).broadcast_to([P, LNT, F]), ALU.subtract).then_inc(s_xc, 1)

            def variance(c):
                t0, t1 = c * LNT, (c + 1) * LNT
                e.wait_ge(s_sq, c + 1)
                link(e.tensor_reduce(mom[:, 2, t0:t1], sq[:, c % 2, :, :], AX, ALU.add))
                e.tensor_scalar(mom[:, 2, t0:t1], mom[:, 2, t0:t1], 1.0 / F, LN_EPS, ALU.mult, ALU.add).then_inc(s_var, 1)

            def scale(c):
                t0, t1 = c * LNT, (c + 1) * LNT
                e.wait_ge(s_dev, c + 1)
                link(e.reciprocal(mom[:, 3, t0:t1], mom[:, 3, t0:t1]))
                e.scalar_tensor_tensor(out=xr[:, t0:t1, :], in0=xr[:, t0:t1, :], scalar=0.0,
                                       in1=mom[:, 3, t0:t1].unsqueeze(2).broadcast_to([P, LNT, F]),
                                       op0=ALU.max, op1=ALU.mult).then_inc(s_ln, 1)

            for c in range(NLN + 2):
                if c < NLN:
                    centre(c)
                if 1 <= c <= NLN:
                    variance(c - 1)
                if c >= 2:
                    scale(c - 2)

            e.wait_ge(s_dst, 16 * 5)
            e.wait_ge(s_idx, 16 * 10)
            for ch, g in ((0, GA), (1, GB)):
                e.tensor_scalar(cls_i[0:g, ch, :], ety_i[0:g, ch, :], int(math.log2(CLS)), None, ALU.logical_shift_right)
                e.tensor_reduce(gstat[0:g, ch, 0:1], dst_i[0:g, ch, :], AX, ALU.min)
                link(e.tensor_reduce(gstat[0:g, ch, 1:2], dst_i[0:g, ch, :], AX, ALU.max))
                e.tensor_scalar(rel_f[0:g, ch, :], dst_i[0:g, ch, :], gstat[0:g, ch, 0:1], None, ALU.subtract)
                e.tensor_tensor(gstat[0:g, ch, 2:3], gstat[0:g, ch, 1:2], gstat[0:g, ch, 0:1], ALU.subtract)
                link(e.scalar_tensor_tensor(out=ety_f[0:g, ch, :], in0=cls_i[0:g, ch, :], scalar=float(CLS * N - CLS),
                                            in1=ety_i[0:g, ch, :], op0=ALU.mult, op1=ALU.add))
                e.scalar_tensor_tensor(out=idx_f[0:g, ch, :], in0=src_i[0:g, ch, :], scalar=float(CLS),
                                       in1=ety_f[0:g, ch, :], op0=ALU.mult, op1=ALU.add).then_inc(s_met, 1)

            def take(n, to_all, ch, g, s_from, s_to):
                e.wait_ge(s_from, n + 1)
                e.tensor_copy(to_all[:, ch * GE:ch * GE + g * GT].rearrange("p (g i) -> p i g", i=GT),
                              mflat.rearrange("p (i g) -> p i g", i=GT)[:, :, 0:g]).then_inc(s_to, 1)

            n = 0
            for ch, g in ((0, GA), (1, GB)):
                for to_all in (idx_all, rel_all, wgt_all):
                    take(n, to_all, ch, g, s_mt, s_me)
                    n += 1
            e.wait_ge(s_mt, 7)
            e.tensor_copy(base_i[:, :], mps[0:1, 0, 0:NG])
            link(e.tensor_reduce(flag_f[:, 0:1], mps[0:1, 1, 0:NG], AX, ALU.max))
            e.tensor_scalar(flag_i[:, :], flag_f[:, 0:1], float(WIN - 1), None, ALU.is_le).then_inc(s_flag, 1)

            flag = fast_path_flag(e)
            with e.If(flag < 1):
                e.tensor_copy(rel_f[0:GA, 0, :], dst_i[0:GA, 0, :])
                e.tensor_copy(rel_f[0:GB, 1, :], dst_i[0:GB, 1, :]).then_inc(s_g["dst"], 1)
                take(0, rel_all, 0, GA, s_g["mt"], s_g["me"])
                take(1, rel_all, 1, GB, s_g["mt"], s_g["me"])
                e.memset(acc[:, :], 0.0)
                for k in range(NZS):
                    e.wait_ge(s_zst[k], 16 * len(range(k, len(STORES), NZS)))
                e.memset(zflat[:, 0:2048], 0.0).then_inc(s_g["zero"], 1)
                e.wait_ge(s_g["me"], 2)
                with e.Fori(0, NTILES) as t:
                    e.tensor_copy(gdst[:, 0:1], rel_all[:, bass.ds(t, 1)])
                    e.tensor_copy(gdst[:, 1:2], wgt_all[:, bass.ds(t, 1)]).then_inc(s_g["mul"], 1)
                    e.wait_ge(s_g["mul"], t * 4 + 1)
                    e.tensor_scalar(gdstb[:, :], ones[:, :], gdst[:, 0:1], None, ALU.mult).then_inc(s_g["bcast"], 1)
                    e.wait_ge(s_g["row"], t + 1)
                    e.tensor_scalar(geq[:, :], mps[:, 0, 0:P], gdst[:, 0:1], None, ALU.is_equal).then_inc(s_g["mul"], 1)
                    e.tensor_tensor(gnum[:, 1:2], dumprow[:, :], gdst[:, 0:1], ALU.subtract)
                    e.wait_ge(s_g["mul"], t * 4 + 2)
                    e.scalar_tensor_tensor(out=gjunk[:, :], in0=geq[:, :], scalar=1.0, in1=lower[:, :],
                                           op0=ALU.mult, op1=ALU.mult, accum_out=gnum[:, 0:1]).then_inc(s_g["mul"], 1)
                    e.wait_ge(s_g["mul"], t * 4 + 3)
                    e.tensor_scalar(gnum[:, 2:3], gnum[:, 0:1], 0.0, None, ALU.is_gt).then_inc(s_g["mul"], 1)
                    e.wait_ge(s_g["mul"], t * 4 + 4)
                    e.wait_ge(s_g["add"], t * 16)
                    e.scalar_tensor_tensor(out=gsidx[:, :], in0=gnum[:, 1:2], scalar=gnum[:, 2:3], in1=gdst[:, 0:1],
                                           op0=ALU.mult, op1=ALU.add)
                    e.wait_ge(s_g["y"], t * 16 + 16)
                    e.tensor_scalar(gyn[:, :], gy[:, :], gdst[:, 1:2], None, ALU.mult).then_inc(s_g["tc"], 1)
                    e.wait_ge(s_g["mm"], t + 1)
                    e.tensor_copy(gsum[:, :], mps[:, 1, 0:F]).then_inc(s_g["sum"], 1)
                for q in range(NQ):
                    e.wait_ge(s_g["tp"], q + 1)
                    e.tensor_copy(acc[0:F, 2 * q * P:(2 * q + 1) * P], aps[0:F, q % 2, 0:P])
                    e.tensor_copy(acc[F:P, (2 * q + 1) * P:(2 * q + 2) * P], aps[F:P, q % 2, 0:P]).then_inc(s_g["back"], 1)
                e.engine_nop().then_inc(s_sum, 1)
            with e.Else():
                e.memset(acc[:, :], 0.0).then_inc(s_acc, 1)

                def add_up(g):
                    base = e.value_load(base_i[0:1, g:g + 1], min_val=0, max_val=N - 1)
                    e.wait_ge(s_agg, min((g + 1) * GT, NTILES))
                    e.wait_ge(s_acc, g + 1)
                    win = acc[:, bass.ds(base, WIN)]
                    e.tensor_tensor(win, win, aps[:, g % 2, 0:WIN], ALU.add).then_inc(s_acc, 1)

                for t in range(NTILES):
                    if t >= NOH:
                        e.wait_ge(s_agg, t - NOH + 1)
                    e.tensor_scalar(oh[:, t % NOH, :], iota[:, :], rel_all[:, t:t + 1], wgt_all[:, t:t + 1],
                                    ALU.is_equal, ALU.mult).then_inc(s_oh, 1)
                    if t % GT == GT - 1 and t >= GT:
                        add_up(t // GT - 1)
                for g in range(NTILES // GT - 1, NG):
                    add_up(g)
                e.wait_ge(s_acc, NG + 1)
                e.engine_nop().then_inc(s_sum, 1)

            for n, (c0, w) in enumerate(ECH):
                e.wait_ge(s_er, n + 1)
                e.wait_ge(s_eh, n + 1)
                e.tensor_tensor(acc[0:F, c0:c0 + w], acc[0:F, c0:c0 + w], res_t[:, n % 2, 0:w], ALU.add).then_inc(s_ey, 1)
            e.wait_ge(s_ey, len(ECH))
            bw = N // BC
            for n in range(BC):
                last = e.bn_stats(bst[:, n, :], acc[0:F, n * bw:(n + 1) * bw])
            last.then_inc(s_ey, 1)
            e.wait_ge(s_ey, len(ECH) + 1)
            e.bn_aggr(bmv[:, 0:2], bst[:, :, :].rearrange("p a b -> p (a b)")).then_inc(s_ey, 1)
            e.wait_ge(s_ey, len(ECH) + 2)
            e.tensor_scalar(bmv[:, 2:3], bmv[:, 1:2], BN_EPS, None, ALU.add).then_inc(s_diag, 1)
            e.memset(acc[F:F + 1, 0:NT * P], 1.0)
            e.wait_ge(s_diag, 2)
            e.reciprocal(bmv[:, 4:5], bmv[:, 3:4]).then_inc(s_ey, 1)
            e.wait_ge(s_ey, len(ECH) + 3)
            e.tensor_tensor(bmv[:, 5:6], bmv[:, 4:5], cols[:, 2:3], ALU.mult).then_inc(s_ey, 1)
            e.wait_ge(s_ey, len(ECH) + 4)
            e.tensor_tensor(bmv[:, 6:7], bmv[:, 0:1], bmv[:, 5:6], ALU.mult).then_inc(s_ey, 1)
            e.tensor_scalar(diag[0:F, :], ident[0:F, 0:F], bmv[:, 5:6], None, ALU.mult)
            e.wait_ge(s_ey, len(ECH) + 5)
            e.tensor_tensor(bmv[:, 7:8], cols[:, 3:4], bmv[:, 6:7], ALU.subtract).then_inc(s_ey, 1)
            for n, t0 in enumerate(range(0, NT, 8)):
                k = min(8, NT - t0)
                e.wait_ge(s_o, n + 1)
                e.tensor_tensor(xs[:, t0:t0 + k, :], xs[:, t0:t0 + k, :],
                                zps[:, n % NZB, 0:k * F].rearrange("p (t f) -> p t f", f=F), ALU.add).then_inc(s_oc, 1)

        @block.tensor
        def _(e):
            e.wait_ge(s_cst, 5)
            e.wait_ge(s_small, 16 * 7)

            def transpose(to, frm, k):
                return e.matmul(to, lhsT=frm, rhs=ident[0:k, 0:k], is_transpose=True, start=True, stop=True)

            def bank(job):
                if job >= NZB:
                    e.wait_ge(s_ez, job - NZB + 1)
                return zps[:, job % NZB, :]

            transpose(bank(0)[0:R, 0:R], comp_sb[:, :], R).then_inc(s_pz, 1)
            transpose(bank(1)[:, 0:F], resw_sb[:, :], F).then_inc(s_pz, 1)
            e.wait_ge(s_basis, 16)
            e.wait_ge(s_ez, 1)
            for n in range(F // CLS):
                b = bank(J_W + n)
                for o in range(CLS):
                    for h in range(2):
                        last = e.matmul(b[h * F:(h + 1) * F, o * R:(o + 1) * R], lhsT=basis_sb[:, :, n * CLS + o],
                                        rhs=compT[:, :], start=True, stop=True)
                last.then_inc(s_pz, 1)
            for n in range(NXJ):
                b = bank(J_X + n)
                q0, q1 = 4 * n, min(4 * n + 4, NQ)
                e.wait_ge(s_ln, math.ceil(2 * q1 / LNT))
                for q in range(q0, q1):
                    last = transpose(b[:, (q - q0) * P:(q - q0 + 1) * P],
                                     xr[:, 2 * q:2 * q + 2, :].rearrange("p t f -> p (t f)"), P)
                last.then_inc(s_pz, 1)

            def edges(ch, g, frm, s_free, n, s_to):
                if n:
                    e.wait_ge(s_free, n)
                for i in range(GT):
                    last = transpose(mflat[:, i * P:i * P + g], frm[0:g, ch, i * P:(i + 1) * P], g)
                last.then_inc(s_to, 1)

            e.wait_ge(s_wgt, 16 * 4)
            n = 0
            for ch, g in ((0, GA), (1, GB)):
                e.wait_ge(s_met, ch + 1)
                for frm in (idx_f, rel_f, wgt_f):
                    edges(ch, g, frm, s_me, n, s_mt)
                    n += 1
            e.wait_ge(s_me, 6)
            for k, b in ((0, 0), (2, 1)):
                transpose(mps[0:1, b, 0:GA], gstat[:, 0, k:k + 1], GA)
                last = transpose(mps[0:1, b, GA:NG], gstat[0:GB, 1, k:k + 1], GB)
            last.then_inc(s_mt, 1)

            job = J_Z
            for c in range(NCLS):
                for t in range(NT):
                    b = bank(job)
                    if c == 0 and t % 8 == 0:
                        e.wait_ge(s_ez, J_X + t // 8 + 1)
                    h = (t % 2) * F
                    e.matmul(b, lhsT=xnT[h:h + F, t // 2, :],
                             rhs=w_sb[h:h + F, c * CLS:(c + 1) * CLS, :].rearrange("p r f -> p (r f)"),
                             start=True, stop=True).then_inc(s_pz, 1)
                    job += 1

            flag = fast_path_flag(e)
            with e.If(flag < 1):
                e.wait_ge(s_g["dst"], 1)
                edges(0, GA, rel_f, s_g["me"], 0, s_g["mt"])
                edges(1, GB, rel_f, s_g["me"], 1, s_g["mt"])
                e.wait_ge(s_g["me"], 2)
                with e.Fori(0, NTILES) as t:
                    e.wait_ge(s_g["bcast"], t + 1)
                    transpose(mps[:, 0, 0:P], gdstb[:, :], P).then_inc(s_g["row"], 1)
                    e.wait_ge(s_g["tc"], t + 1)
                    e.matmul(mps[:, 1, 0:F], lhsT=geq[:, :], rhs=gyn[:, :], start=True, stop=True).then_inc(s_g["mm"], 1)
                e.wait_ge(s_g["back"], 16)
                for q in range(NQ):
                    if q >= 2:
                        e.wait_ge(s_g["back"], 16 + q - 1)
                    transpose(aps[:, q % 2, 0:P], xr[:, 2 * q:2 * q + 2, :].rearrange("p t f -> p (t f)"), P).then_inc(s_g["tp"], 1)
            with e.Else():
                for t in range(NTILES):
                    g, i = divmod(t, GT)
                    if i == 0 and g >= 2:
                        e.wait_ge(s_acc, g)
                    e.wait_ge(s_y[t % NY], 16 * (t // NY + 1))
                    e.wait_ge(s_oh, t + 1)
                    h = (i % 2) * F
                    e.matmul(aps[h:h + F, g % 2, 0:WIN], lhsT=ys[:, t % NY, :], rhs=oh[:, t % NOH, :],
                             start=(i < 2), stop=(i >= GT - 2 or t >= NTILES - 2)).then_inc(s_agg, 1)

            e.wait_ge(s_sum, 1)
            for n, (c0, w) in enumerate(ECH):
                if n >= 2:
                    e.wait_ge(s_eh, n - 1)
                    e.wait_ge(s_er, n - 1)
                e.matmul(aps[0:F, n % 2, 0:w], lhsT=stack2[:, :], rhs=acc[:, c0:c0 + w], start=True, stop=True)
                q0 = c0 // (2 * P)
                q1 = min(q0 + 2, NQ)
                for h in range(2):
                    last = e.matmul(zps[0:F, 2 * (n % 2) + h, 0:(q1 - q0) * P], lhsT=reswT[h * F:(h + 1) * F, :],
                                    rhs=xnT[h * F:(h + 1) * F, q0:q1, :].rearrange("p q n -> p (q n)"),
                                    start=True, stop=True)
                last.then_inc(s_e1, 1)
            e.wait_ge(s_ey, len(ECH) + 6)
            e.matmul(mps[F:F + 1, 0, 0:F], lhsT=bmv[:, 7:8], rhs=ident[0:F, 0:F], start=True, stop=True).then_inc(s_sh, 1)
            e.wait_ge(s_shc, 1)
            for n, t0 in enumerate(range(0, NT, 8)):
                if n >= NZB:
                    e.wait_ge(s_oc, n - NZB + 1)
                for t in range(t0, min(t0 + 8, NT)):
                    last = e.matmul(zps[:, n % NZB, (t - t0) * F:(t - t0 + 1) * F], lhsT=acc[0:F + 1, t * P:(t + 1) * P],
                                    rhs=diag[:, :], start=True, stop=True)
                last.then_inc(s_o, 1)


_INS = ["x", "src", "dst", "edge_type_64", "edge_weight1", "L0_gnn_basis", "L0_gnn_comp", "L0_gnn_bias",
        "L0_gnn_res_w", "L0_gnn_res_b", "L0_gnn_gamma", "L0_gnn_beta"]


def kernel(**inputs):
    import numpy as np
    import concourse.bacc as bacc
    from concourse.bass_utils import run_bass_kernel_spmd

    nc = bacc.Bacc("TRN2", target_bir_lowering=False, num_devices=1)
    arrays, args = {}, []
    for name in _INS:
        a = np.ascontiguousarray(inputs[name])
        if name == "edge_weight1":
            a = a.reshape(-1)
        arrays[f"in_{name}"] = a
        args.append(nc.dram_tensor(f"in_{name}", a.shape, mybir.dt.from_np(a.dtype), kind="ExternalInput").ap())
    shape = inputs["x"].shape
    args.append(nc.dram_tensor("out_x", shape, F32, kind="ExternalOutput").ap())
    rgcn_kernel(nc, *args)
    r = run_bass_kernel_spmd(nc, [arrays], core_ids=[0])
    return r.results[0]["out_x"]
```

```python
import math
from contextlib import ExitStack

import concourse.bass as bass
from concourse import mybir

F32 = mybir.dt.float32
I32 = mybir.dt.int32
BF16 = mybir.dt.bfloat16
ALU = mybir.AluOpType
ACT = mybir.ActivationFunctionType
AX = mybir.AxisListType.X

P = 128
BANK = 512
LN_EPS = 1e-5
BN_EPS = 1e-5
GT = 8
GE = GT * P
WIN = 192
CLS = 8
NZB = 4
ZT = 4
NZS = 4
NY = 16
NOH = 8
LNT = 14


def rgcn_kernel(nc, x, src, dst, etype, weight, basis, comp, bias, res_w, res_b, gamma, beta, out):
    N, F = x.shape
    E = src.shape[0]
    R = comp.shape[0]
    NT = math.ceil(N / P)
    LAST = N - (NT - 1) * P
    NQ = NT // 2
    NCH = math.ceil(NT * P / BANK)
    NCLS = R // CLS
    NG = math.ceil(E / GE)
    LE = E - (NG - 1) * GE
    NTILES = math.ceil(E / P)
    GA, GB = P, NG - P
    NLN = NT // LNT
    assert NLN + 2 == F // CLS + 1 and NT % 2 == 0 and NT % LNT == 0 and CLS * F == BANK and 64 < GB <= P and F == 64 and R == 64
    DUMP = NT * P
    ROWS = DUMP + P

    table = nc.dram_tensor("z_table", [NCLS * N * CLS, F], F32)
    accd = nc.dram_tensor("acc_rows", [ROWS, F], F32)

    with ExitStack() as ctx:
        def sb(name, shape, dt=F32):
            return ctx.enter_context(nc.sbuf_tensor(name, shape, dt))

        def sem(name):
            return ctx.enter_context(nc.semaphore(name))

        ARENA = NT * P + WIN + 16
        acc = sb("acc", [P, ARENA])
        ar_f = acc[:, 0:6 * 2 * GE].rearrange("p (a c n) -> p a c n", a=6, c=2)
        ar_i = acc[:, 0:6 * 2 * GE].bitcast(I32).rearrange("p (a c n) -> p a c n", a=6, c=2)
        dst_i, src_i, ety_i, cls_i = (ar_i[:, k] for k in range(4))
        idx_f, ety_f = ar_f[:, 1], ar_f[:, 2]
        rel_f, wgt_f = ar_f[:, 4], ar_f[:, 5]
        res = sb("res", [P, NCH, BANK])
        xp = res[:, :, :].bitcast(BF16).rearrange("p c (a n) -> p c a n", a=2)
        basis_sb = res[0:R, 0:F * F // BANK, :].rearrange("b q n -> b (q n)").rearrange("b (i o) -> b i o", o=F)
        xr = res[:, :, :].rearrange("p c n -> p (c n)")[:, NCH * BANK - NT * F:].rearrange("p (t f) -> p t f", f=F)
        wp = sb("wp", [P, 3, R + 1, F], BF16)
        shared = sb("shared", [P, 2 * LNT * F + 4 * BANK])
        xdup = shared[:, 0:2 * BANK].rearrange("p (s t a f) -> p s t a f", s=2, a=2, f=F)
        rem = shared[:, 2 * BANK:4 * BANK].rearrange("p (s n) -> p s n", s=2)
        sq = shared[:, 4 * BANK:4 * BANK + 2 * LNT * F].rearrange("p (s t f) -> p s t f", s=2, f=F)
        ys = shared[:, 0:NY * F].rearrange("p (s f) -> p s f", f=F)
        oh = shared[:, NY * F:NY * F + NOH * WIN].rearrange("p (s n) -> p s n", n=WIN)
        gdstb, geq, gjunk = (shared[:, k * P:(k + 1) * P] for k in range(3))
        x2l = sb("x2l", [F, BANK], BF16)
        zst = sb("zst", [P, NZS, ZT, BANK])
        zflat = zst[:, :, :, :].rearrange("p s t n -> p (s t n)")
        xo = zflat[:, 0:NT * F].rearrange("p (t f) -> p t f", f=F)
        mom = sb("mom", [P, 4, NT])
        idx_all = sb("idx_all", [P, NG * GT], I32)
        rel_all = sb("rel_all", [P, NG * GT])
        wgt_all = sb("wgt_all", [P, NG * GT])
        ident = sb("ident", [P, P])
        stack2 = sb("stack2", [P, F])
        ones = sb("ones", [P, P])
        lower = sb("lower", [P, P])
        iota = sb("iota", [P, WIN])
        dumprow = sb("dumprow", [P, 1])
        comp_sb = sb("comp_sb", [R, R])
        compT = sb("compT", [R, R])
        resw_sb = sb("resw_sb", [F, 2 * F])
        cols = sb("cols", [F, 4])
        gstat = sb("gstat", [P, 2, 3])
        base_i = sb("base_i", [1, NG], I32)
        span_r = sb("span_r", [1, NG])
        flag_f = sb("flag_f", [1, 2])
        flag_i = sb("flag_i", [1, 1], I32)
        BC = 25
        bst = sb("bst", [F, BC, 6])
        bmv = sb("bmv", [F, 8])
        diag = sb("diag", [F + 1, F])
        gdst = sb("gdst", [P, 2])
        gnum = sb("gnum", [P, 4])
        gidx = sb("gidx", [P, 1], I32)
        gsidx = sb("gsidx", [P, 1], I32)
        gy = sb("gy", [P, F])
        gyn = sb("gyn", [P, F])
        gsum = sb("gsum", [P, F])

        zps = ctx.enter_context(nc.psum_tensor("zps", [P, NZB, BANK], F32))
        aps = ctx.enter_context(nc.psum_tensor("aps", [P, 2, BANK], F32))
        mps = ctx.enter_context(nc.psum_tensor("mps", [P, 2, BANK], F32))
        mflat = mps[:, :, :].rearrange("p b n -> p (b n)")

        s_x = [sem(f"s_x{c}") for c in range(NLN)]
        s_small, s_basis = sem("s_small"), sem("s_basis")
        s_dst, s_idx, s_wgt = sem("s_dst"), sem("s_idx"), sem("s_wgt")
        s_pad = sem("s_pad")
        s_cst, s_pc = sem("s_cst"), sem("s_pc")
        s_xc, s_sq, s_var, s_dev, s_ln = (sem(n) for n in ("s_xc", "s_sq", "s_var", "s_dev", "s_ln"))
        s_pz, s_ez, s_ed = sem("s_pz"), sem("s_ez"), sem("s_ed")
        s_p1, s_rem, s_p2 = sem("s_p1"), sem("s_rem"), sem("s_p2")
        s_dup = sem("s_dup")
        s_xo, s_xre = sem("s_xo"), sem("s_xre")
        s_zst = [sem(f"s_zst{k}") for k in range(NZS)]
        s_met, s_mt, s_me = sem("s_met"), sem("s_mt"), sem("s_me")
        s_flag = sem("s_flag")
        s_y = [sem(f"s_y{k}") for k in range(NY)]
        s_oh, s_agg, s_acc = sem("s_oh"), sem("s_agg"), sem("s_acc")
        s_dv = sem("s_dv")
        s_sum = sem("s_sum")
        s_g = {k: sem(f"s_g_{k}") for k in
               ("dst", "mt", "me", "zero", "clr", "bcast", "row", "idx", "y", "mul", "mm", "sum", "add", "back", "tp", "tc", "go")}
        s_e1, s_er, s_eh, s_ey = sem("s_e1"), sem("s_er"), sem("s_eh"), sem("s_ey")
        s_diag, s_sh, s_shc, s_o, s_oc, s_out = (sem(n) for n in ("s_diag", "s_sh", "s_shc", "s_o", "s_oc", "s_out"))

        AHEAD = 2
        jobs = [("comp",), ("resw",)] + [("w", n) for n in range(F // CLS)]
        for c in range(NCH + AHEAD):
            jobs += [("x", c)] if c < NCH else []
            jobs += [("z", 0, t) for t in range((c - AHEAD) * 4, min((c - AHEAD + 1) * 4, NT)) if c >= AHEAD]
        jobs += [("z", c, t) for c in range(1, NCLS) for t in range(NT)]
        jobs += [("r", c) for c in range(NCH)]
        at = {job: n for n, job in enumerate(jobs)}
        nth = {}
        emptied = {s_ez: 0, s_ed: 0}
        for job in jobs:
            by = s_ez if job[0] in ("comp", "z", "r") else s_ed
            emptied[by] += 1
            nth[job] = (by, emptied[by])
        splits = [job for job in jobs if nth[job][0] is s_ed]
        X0 = splits.index(("x", 0))

        def bank_of(job):
            return zps[:, at[job] % NZB, :]

        ZG = [(t, min(ZT, NT - 1 - t)) for t in range(0, NT - 1, ZT)] + [(NT - 1, 1)]
        STORES = [(c, t0, k) for c in range(NCLS) for t0, k in ZG]
        zview = table[:, :].rearrange("(c n r) f -> c n (r f)", c=NCLS, r=CLS)
        ECH = [(c, min(BANK, N - c)) for c in range(0, N, BANK)]

        def evac_done_of_store(n):
            return 1 + sum(k for _, _, k in STORES[:n + 1])

        def fast_path_flag(e):
            e.wait_ge(s_flag, 1)
            return e.value_load(flag_i[0:1, 0:1], min_val=0, max_val=1)

        block = ctx.enter_context(nc.Block())

        @block.sync
        def _(e):
            xv = x[0:(NT - 1) * P, :].rearrange("(t p) f -> p t f", p=P)
            for c in range(NLN):
                t0, t1 = c * LNT, min((c + 1) * LNT, NT - 1)
                e.dma_start(xr[:, t0:t1, :], xv[:, t0:t1, :]).then_inc(s_x[c], 16)
            e.wait_ge(s_pad, 1)
            e.dma_start(xr[0:LAST, NT - 1, :], x[(NT - 1) * P:N, :]).then_inc(s_x[NLN - 1], 16)
            for n, (c, t0, k) in enumerate(STORES):
                e.wait_ge(s_ez, evac_done_of_store(n))
                rows = LAST if t0 == NT - 1 else P
                e.dma_start(zview[c, t0 * P:t0 * P + (k - 1) * P + rows, :].rearrange("(t p) w -> p t w", p=rows),
                            zst[0:rows, n % NZS, 0:k, :]).then_inc(s_zst[n % NZS], 16)
            flag = fast_path_flag(e)
            with e.If(flag < 1):
                e.wait_ge(s_g["zero"], 1)
                av = accd[:, :].rearrange("(p t) f -> p (t f)", p=P)
                width = ROWS // P * F
                cuts = list(range(0, width, 2048)) + [width]
                for a, b in zip(cuts, cuts[1:]):
                    e.dma_start(av[:, a:b], zflat[:, 0:b - a]).then_inc(s_g["clr"], 16)
                e.wait_ge(s_g["add"], 16 * NTILES)
                e.wait_ge(s_g["clr"], 16 * (len(cuts) - 1))
                e.dma_start(xo, accd[0:NT * P, :].rearrange("(t p) f -> p t f", p=P)).then_inc(s_g["back"], 16)
                e.wait_ge(s_sum, 1)
            for k in range(NZS):
                e.wait_ge(s_zst[k], 16 * len(range(k, len(STORES), NZS)))
            e.dma_start(xo[:, 0:NT - 1, :], xv).then_inc(s_xre, 16)
            e.dma_start(xo[0:LAST, NT - 1, :], x[(NT - 1) * P:N, :]).then_inc(s_xre, 16)
            ov = out[0:(NT - 1) * P, :].rearrange("(t p) f -> p t f", p=P)
            for n, t0 in enumerate(range(0, NT, 8)):
                t1 = min(t0 + 8, NT - 1)
                e.wait_ge(s_oc, n + 1)
                e.dma_start(ov[:, t0:t1, :], xo[:, t0:t1, :]).then_inc(s_out, 16)
            e.dma_start(out[(NT - 1) * P:N, :], xo[0:LAST, NT - 1, :]).then_inc(s_out, 16)
            e.wait_ge(s_out, 16 * (math.ceil(NT / 8) + 1))

        @block.gpsimd
        def _(e):
            e.memset(ident[:, :], 0.0).then_inc(s_pc, 1)
            e.memset(stack2[:, :], 0.0).then_inc(s_pc, 1)
            e.memset(lower[:, :], 0.0).then_inc(s_pc, 1)
            e.memset(ones[:, :], 1.0)
            e.wait_ge(s_pc, 3)
            e.affine_select(out=ident[:, :], in_=ident[:, :], compare_op=ALU.not_equal, fill=1.0,
                            base=0, pattern=[[-1, P]], channel_multiplier=1).then_inc(s_cst, 1)
            e.affine_select(out=lower[:, :], in_=lower[:, :], compare_op=ALU.is_ge, fill=1.0,
                            base=0, pattern=[[1, P]], channel_multiplier=-1).then_inc(s_cst, 1)
            e.affine_select(out=stack2[:, :], in_=stack2[:, :], compare_op=ALU.not_equal, fill=1.0,
                            base=0, pattern=[[-1, F]], channel_multiplier=1).then_inc(s_pc, 1)
            e.wait_ge(s_pc, 4)
            e.affine_select(out=stack2[:, :], in_=stack2[:, :], compare_op=ALU.not_equal, fill=1.0,
                            base=-F, pattern=[[-1, F]], channel_multiplier=1).then_inc(s_cst, 1)
            e.iota(iota[:, :], [[1, WIN]], base=0, channel_multiplier=0,
                   allow_small_or_imprecise_dtypes=True).then_inc(s_cst, 1)
            e.iota(dumprow[:, :], [[1, 1]], base=DUMP, channel_multiplier=1,
                   allow_small_or_imprecise_dtypes=True).then_inc(s_cst, 1)
            for c in range(NCH):
                t0, t1 = c * BANK // P, min((c + 1) * BANK // P, NT)
                e.wait_ge(s_ln, math.ceil(t1 / LNT))
                if c >= 2:
                    e.wait_ge(s_pz, at["x", c - 2] + 1)
                e.tensor_copy(xdup[:, c % 2, 0:t1 - t0, :, :],
                              xr[:, t0:t1, :].unsqueeze(2).broadcast_to([P, t1 - t0, 2, F])).then_inc(s_dup, 1)
            for k in range(NZS):
                e.wait_ge(s_zst[k], 16 * len(range(k, len(STORES), NZS)))
            flag = fast_path_flag(e)
            with e.If(flag < 1):
                e.wait_ge(s_g["clr"], 16 * math.ceil(ROWS // P * F / 2048))
                with e.Fori(0, NTILES) as t:
                    e.tensor_copy(gidx[:, :], idx_all[:, bass.ds(t, 1)]).then_inc(s_g["idx"], 1)
                    e.wait_ge(s_g["idx"], t + 1)
                    e.sem_inc(s_g["go"], 1)
                    e.indirect_dma_start(out=gy[:, :], out_offset=None, in_=table[:, :],
                                         in_offset=bass.IndirectOffsetOnAxis(ap=gidx[:, :], axis=0)).then_inc(s_g["y"], 16)
                    e.wait_ge(s_g["sum"], t + 1)
                    e.sem_inc(s_g["go"], 1)
                    e.indirect_dma_start(out=accd[:, :], out_offset=bass.IndirectOffsetOnAxis(ap=gsidx[:, :], axis=0),
                                         in_=gsum[:, :], in_offset=None, compute_op=ALU.add).then_inc(s_g["add"], 16)
                    e.wait_ge(s_g["add"], t * 16 + 16)
            with e.Else():
                for t in range(NTILES):
                    if t >= NY:
                        e.wait_ge(s_agg, t - NY + 1)
                    e.indirect_dma_start(out=ys[:, t % NY, :], out_offset=None, in_=table[:, :],
                                         in_offset=bass.IndirectOffsetOnAxis(ap=idx_all[:, t:t + 1], axis=0)
                                         ).then_inc(s_y[t % NY], 16)

        @block.scalar
        def _(e):
            e.dma_start(comp_sb[:, :], comp).then_inc(s_small, 16)
            e.dma_start(resw_sb[:, 0:F], res_w).then_inc(s_small, 16)
            e.dma_start(resw_sb[:, F:2 * F], res_w).then_inc(s_small, 16)
            e.dma_start(basis_sb, basis).then_inc(s_basis, 16)
            for k, v in enumerate((bias, res_b, gamma, beta)):
                e.dma_start(cols[:, k:k + 1], v.rearrange("(f a) -> f a", a=1)).then_inc(s_small, 16)
            e.wait_ge(s_pad, 2)
            for arr, to, s in ((dst, dst_i, s_dst), (src, src_i, s_idx), (etype, ety_i, s_idx), (weight, wgt_f, s_wgt)):
                e.dma_start(to[:, 0, :], arr[0:P * GE].rearrange("(g n) -> g n", n=GE)).then_inc(s, 16)
                e.dma_start(to[0:64, 1, :], arr[P * GE:(P + 64) * GE].rearrange("(g n) -> g n", n=GE)).then_inc(s, 16)
                e.dma_start(to[64:GB - 1, 1, :], arr[(P + 64) * GE:(NG - 1) * GE].rearrange("(g n) -> g n", n=GE)).then_inc(s, 16)
                e.dma_start(to[GB - 1:GB, 1, 0:LE], arr[E - LE:E].rearrange("(g n) -> g n", n=LE)).then_inc(s, 16)
                if arr is not weight:
                    e.dma_start(to[GB - 1:GB, 1, LE:GE], arr[E - (GE - LE):E].rearrange("(g n) -> g n", n=GE - LE)).then_inc(s, 16)

            def take(job, to, frm):
                e.wait_ge(s_pz, at[job] + 1)
                e.activation(to, frm, ACT.Copy).then_inc(s_ez, 1)

            def square(c):
                e.wait_ge(s_xc, c + 1)
                if c >= 2:
                    e.wait_ge(s_var, c - 1)
                e.activation(sq[:, c % 2, :, :], xr[:, c * LNT:(c + 1) * LNT, :], ACT.Square).then_inc(s_sq, 1)

            def deviation(c):
                e.wait_ge(s_var, c + 1)
                e.activation(mom[:, 3, c * LNT:(c + 1) * LNT], mom[:, 2, c * LNT:(c + 1) * LNT], ACT.Sqrt).then_inc(s_dev, 1)

            def first_part(n):
                kind, *c = splits[n]
                b = bank_of(splits[n])
                e.wait_ge(s_pz, at[splits[n]] + 1)
                if kind == "resw":
                    to, frm = wp[:, 0, R, :], b[:, 0:F]
                elif kind == "w":
                    to, frm = wp[:, 0, 0:R, c[0] * CLS:(c[0] + 1) * CLS], b.rearrange("p (o r) -> p r o", r=R)
                else:
                    w = min(BANK, NT * P - c[0] * BANK)
                    to, frm = xp[:, c[0], 1, 0:w], b[:, 0:w]
                e.activation(to, frm, ACT.Copy).then_inc(s_p1, 1)

            def second_part(c):
                n = X0 + c
                w = min(BANK, NT * P - c * BANK)
                e.wait_ge(s_rem, n + 1)
                e.activation(xp[F:P, c, 0, 0:w], rem[F:P, n % 2, 0:w], ACT.Copy).then_inc(s_p2, 1)

            def products(n):
                c, t0, k = STORES[n]
                rows = LAST if t0 == NT - 1 else P
                if n >= NZS:
                    e.wait_ge(s_zst[n % NZS], 16 * (n // NZS))
                for i in range(k):
                    take(("z", c, t0 + i), zst[0:rows, n % NZS, i, :], bank_of(("z", c, t0 + i))[0:rows, :])

            take(("comp",), compT[:, :], bank_of(("comp",))[0:R, 0:R])
            for n in range(X0):
                first_part(n)
                if n < NLN:
                    square(n)
                if 1 <= n <= NLN:
                    deviation(n - 1)
            for c in range(NCH + 2):
                if c < NCH:
                    first_part(X0 + c)
                if 1 <= c <= NCH:
                    second_part(c - 1)
                if c >= 2:
                    products(c - 2)
            for n in range(NCH, len(STORES)):
                products(n)
            for c in range(NCH):
                w = min(BANK, NT * P - c * BANK)
                e.wait_ge(s_pz, at["r", c] + 1)
                e.activation(res[0:F, c, 0:w], bank_of(("r", c))[0:F, 0:w], ACT.Relu, bias=cols[:, 1:2]).then_inc(s_ez, 1)

            for n, (c0, w) in enumerate(ECH):
                e.wait_ge(s_e1, n + 1)
                e.activation(acc[0:F, c0:c0 + w], aps[0:F, n % 2, 0:w], ACT.Relu, bias=cols[:, 0:1]).then_inc(s_eh, 1)
            e.wait_ge(s_diag, 1)
            e.activation(bmv[:, 3:4], bmv[:, 2:3], ACT.Sqrt).then_inc(s_diag, 1)
            e.wait_ge(s_sh, 1)
            e.activation(diag[F:F + 1, :], mps[F:F + 1, 0, 0:F], ACT.Copy).then_inc(s_shc, 1)

        @block.vector
        def _(e):
            steps = [0]

            def link(ins):
                steps[0] += 1
                ins.then_inc(s_dv, 1)
                e.wait_ge(s_dv, steps[0])

            e.memset(xr[:, NT - 1, :], 0.0).then_inc(s_pad, 1)
            e.memset(wgt_f[64:GB, 1, :], 0.0).then_inc(s_pad, 1)
            def centre(c):
                t0, t1 = c * LNT, (c + 1) * LNT
                e.wait_ge(s_x[c], 32 if c == NLN - 1 else 16)
                link(e.tensor_reduce(mom[:, 0, t0:t1], xr[:, t0:t1, :], AX, ALU.add))
                link(e.tensor_scalar(mom[:, 1, t0:t1], mom[:, 0, t0:t1], 1.0 / F, None, ALU.mult))
                e.tensor_tensor(xr[:, t0:t1, :], xr[:, t0:t1, :],
                                mom[:, 1, t0:t1].unsqueeze(2).broadcast_to([P, LNT, F]), ALU.subtract).then_inc(s_xc, 1)

            def variance(c):
                t0, t1 = c * LNT, (c + 1) * LNT
                e.wait_ge(s_sq, c + 1)
                link(e.tensor_reduce(mom[:, 2, t0:t1], sq[:, c % 2, :, :], AX, ALU.add))
                e.tensor_scalar(mom[:, 2, t0:t1], mom[:, 2, t0:t1], 1.0 / F, LN_EPS, ALU.mult, ALU.add).then_inc(s_var, 1)

            def scale(c):
                t0, t1 = c * LNT, (c + 1) * LNT
                e.wait_ge(s_dev, c + 1)
                link(e.reciprocal(mom[:, 3, t0:t1], mom[:, 3, t0:t1]))
                e.scalar_tensor_tensor(out=xr[:, t0:t1, :], in0=xr[:, t0:t1, :], scalar=0.0,
                                       in1=mom[:, 3, t0:t1].unsqueeze(2).broadcast_to([P, LNT, F]),
                                       op0=ALU.max, op1=ALU.mult).then_inc(s_ln, 1)

            def split(n):
                kind, *c = splits[n]
                b = bank_of(splits[n])
                if n >= 2:
                    e.wait_ge(s_p2, n - 1)
                e.wait_ge(s_p1, n + 1)
                if kind != "x":
                    if kind == "resw":
                        k, o0, o1, frm = slice(R, R + 1), 0, F, b[:, 0:F].unsqueeze(1)
                        r_all = rem[:, n % 2, 0:F].unsqueeze(1)
                    else:
                        k, o0, o1 = slice(0, R), c[0] * CLS, (c[0] + 1) * CLS
                        frm = b.rearrange("p (o r) -> p r o", r=R)
                        r_all = rem[:, n % 2, :].rearrange("p (o r) -> p r o", r=R)
                    e.tensor_tensor(r_all, frm, wp[:, 0, k, o0:o1], ALU.subtract).then_inc(s_rem, 1)
                    e.tensor_copy(wp[0:F, 2, k, o0:o1], wp[0:F, 0, k, o0:o1])
                    e.wait_ge(s_rem, n + 1)
                    link(e.tensor_copy(wp[:, 1, k, o0:o1], r_all))
                    e.tensor_tensor(wp[F:P, 2, k, o0:o1], r_all[F:P], wp[F:P, 1, k, o0:o1], ALU.subtract).then_inc(s_p2, 1)
                    e.sem_inc(s_ed, 1)
                else:
                    c = c[0]
                    w = min(BANK, NT * P - c * BANK)
                    e.tensor_tensor(rem[:, n % 2, 0:w], b[:, 0:w], xp[:, c, 1, 0:w], ALU.subtract).then_inc(s_rem, 1)
                    e.tensor_copy(xp[0:F, c, 0, 0:w], xp[0:F, c, 1, 0:w]).then_inc(s_ed, 1)
                    e.wait_ge(s_rem, n + 1)
                    link(e.tensor_copy(x2l[:, 0:w], rem[0:F, n % 2, 0:w]))
                    e.tensor_tensor(xp[0:F, c, 1, 0:w], rem[0:F, n % 2, 0:w], x2l[:, 0:w], ALU.subtract).then_inc(s_xo, 1)

            for c in range(NLN + 2):
                if c < NLN:
                    centre(c)
                if 1 <= c <= NLN:
                    variance(c - 1)
                if c >= 2:
                    scale(c - 2)
                split(c)
            for n in range(NLN + 2, len(splits)):
                split(n)

            e.wait_ge(s_dst, 16 * 5)
            e.wait_ge(s_idx, 16 * 10)
            for ch, g in ((0, GA), (1, GB)):
                e.tensor_scalar(cls_i[0:g, ch, :], ety_i[0:g, ch, :], int(math.log2(CLS)), None, ALU.logical_shift_right)
                e.tensor_reduce(gstat[0:g, ch, 0:1], dst_i[0:g, ch, :], AX, ALU.min)
                link(e.tensor_reduce(gstat[0:g, ch, 1:2], dst_i[0:g, ch, :], AX, ALU.max))
                e.tensor_scalar(rel_f[0:g, ch, :], dst_i[0:g, ch, :], gstat[0:g, ch, 0:1], None, ALU.subtract)
                e.tensor_tensor(gstat[0:g, ch, 2:3], gstat[0:g, ch, 1:2], gstat[0:g, ch, 0:1], ALU.subtract)
                link(e.scalar_tensor_tensor(out=ety_f[0:g, ch, :], in0=cls_i[0:g, ch, :], scalar=float(CLS * N - CLS),
                                            in1=ety_i[0:g, ch, :], op0=ALU.mult, op1=ALU.add))
                e.scalar_tensor_tensor(out=idx_f[0:g, ch, :], in0=src_i[0:g, ch, :], scalar=float(CLS),
                                       in1=ety_f[0:g, ch, :], op0=ALU.mult, op1=ALU.add).then_inc(s_met, 1)

            def take(n, to_all, ch, g, s_from, s_to):
                e.wait_ge(s_from, n + 1)
                e.tensor_copy(to_all[:, ch * GE:ch * GE + g * GT].rearrange("p (g i) -> p i g", i=GT),
                              mflat.rearrange("p (i g) -> p i g", i=GT)[:, :, 0:g]).then_inc(s_to, 1)

            n = 0
            for ch, g in ((0, GA), (1, GB)):
                for to_all in (idx_all, rel_all, wgt_all):
                    take(n, to_all, ch, g, s_mt, s_me)
                    n += 1
            e.wait_ge(s_mt, 7)
            e.tensor_copy(base_i[:, :], mps[0:1, 0, 0:NG])
            link(e.tensor_reduce(flag_f[:, 0:1], mps[0:1, 1, 0:NG], AX, ALU.max))
            e.tensor_scalar(flag_i[:, :], flag_f[:, 0:1], float(WIN - 1), None, ALU.is_le).then_inc(s_flag, 1)

            flag = fast_path_flag(e)
            with e.If(flag < 1):
                e.tensor_copy(rel_f[0:GA, 0, :], dst_i[0:GA, 0, :])
                e.tensor_copy(rel_f[0:GB, 1, :], dst_i[0:GB, 1, :]).then_inc(s_g["dst"], 1)
                take(0, rel_all, 0, GA, s_g["mt"], s_g["me"])
                take(1, rel_all, 1, GB, s_g["mt"], s_g["me"])
                e.memset(acc[:, :], 0.0)
                for k in range(NZS):
                    e.wait_ge(s_zst[k], 16 * len(range(k, len(STORES), NZS)))
                e.memset(zflat[:, 0:2048], 0.0).then_inc(s_g["zero"], 1)
                e.wait_ge(s_g["me"], 2)
                with e.Fori(0, NTILES) as t:
                    e.tensor_copy(gdst[:, 0:1], rel_all[:, bass.ds(t, 1)])
                    e.tensor_copy(gdst[:, 1:2], wgt_all[:, bass.ds(t, 1)]).then_inc(s_g["mul"], 1)
                    e.wait_ge(s_g["mul"], t * 4 + 1)
                    e.tensor_scalar(gdstb[:, :], ones[:, :], gdst[:, 0:1], None, ALU.mult).then_inc(s_g["bcast"], 1)
                    e.wait_ge(s_g["row"], t + 1)
                    e.tensor_scalar(geq[:, :], mps[:, 0, 0:P], gdst[:, 0:1], None, ALU.is_equal).then_inc(s_g["mul"], 1)
                    e.tensor_tensor(gnum[:, 1:2], dumprow[:, :], gdst[:, 0:1], ALU.subtract)
                    e.wait_ge(s_g["mul"], t * 4 + 2)
                    e.scalar_tensor_tensor(out=gjunk[:, :], in0=geq[:, :], scalar=1.0, in1=lower[:, :],
                                           op0=ALU.mult, op1=ALU.mult, accum_out=gnum[:, 0:1]).then_inc(s_g["mul"], 1)
                    e.wait_ge(s_g["mul"], t * 4 + 3)
                    e.tensor_scalar(gnum[:, 2:3], gnum[:, 0:1], 0.0, None, ALU.is_gt).then_inc(s_g["mul"], 1)
                    e.wait_ge(s_g["mul"], t * 4 + 4)
                    e.wait_ge(s_g["add"], t * 16)
                    e.scalar_tensor_tensor(out=gsidx[:, :], in0=gnum[:, 1:2], scalar=gnum[:, 2:3], in1=gdst[:, 0:1],
                                           op0=ALU.mult, op1=ALU.add)
                    e.wait_ge(s_g["y"], t * 16 + 16)
                    e.tensor_scalar(gyn[:, :], gy[:, :], gdst[:, 1:2], None, ALU.mult).then_inc(s_g["tc"], 1)
                    e.wait_ge(s_g["mm"], t + 1)
                    e.tensor_copy(gsum[:, :], mps[:, 1, 0:F]).then_inc(s_g["sum"], 1)
                for q in range(NQ):
                    e.wait_ge(s_g["tp"], q + 1)
                    e.tensor_copy(acc[0:F, 2 * q * P:(2 * q + 1) * P], aps[0:F, q % 2, 0:P])
                    e.tensor_copy(acc[F:P, (2 * q + 1) * P:(2 * q + 2) * P], aps[F:P, q % 2, 0:P]).then_inc(s_g["back"], 1)
                e.engine_nop().then_inc(s_sum, 1)
            with e.Else():
                e.memset(acc[:, :], 0.0).then_inc(s_acc, 1)

                def add_up(g):
                    base = e.value_load(base_i[0:1, g:g + 1], min_val=0, max_val=N - 1)
                    e.wait_ge(s_agg, min((g + 1) * GT, NTILES))
                    e.wait_ge(s_acc, g + 1)
                    win = acc[:, bass.ds(base, WIN)]
                    e.tensor_tensor(win, win, aps[:, g % 2, 0:WIN], ALU.add).then_inc(s_acc, 1)

                for t in range(NTILES):
                    if t >= NOH:
                        e.wait_ge(s_agg, t - NOH + 1)
                    e.tensor_scalar(oh[:, t % NOH, :], iota[:, :], rel_all[:, t:t + 1], wgt_all[:, t:t + 1],
                                    ALU.is_equal, ALU.mult).then_inc(s_oh, 1)
                    if t % GT == GT - 1 and t >= GT:
                        add_up(t // GT - 1)
                for g in range(NTILES // GT - 1, NG):
                    add_up(g)
                e.wait_ge(s_acc, NG + 1)
                e.engine_nop().then_inc(s_sum, 1)

            for n, (c0, w) in enumerate(ECH):
                e.wait_ge(s_eh, n + 1)
                e.tensor_tensor(acc[0:F, c0:c0 + w], acc[0:F, c0:c0 + w], res[0:F, n, 0:w], ALU.add).then_inc(s_ey, 1)
            e.wait_ge(s_ey, len(ECH))
            bw = N // BC
            for n in range(BC):
                last = e.bn_stats(bst[:, n, :], acc[0:F, n * bw:(n + 1) * bw])
            last.then_inc(s_ey, 1)
            e.wait_ge(s_ey, len(ECH) + 1)
            e.bn_aggr(bmv[:, 0:2], bst[:, :, :].rearrange("p a b -> p (a b)")).then_inc(s_ey, 1)
            e.wait_ge(s_ey, len(ECH) + 2)
            e.tensor_scalar(bmv[:, 2:3], bmv[:, 1:2], BN_EPS, None, ALU.add).then_inc(s_diag, 1)
            e.memset(acc[F:F + 1, 0:NT * P], 1.0)
            e.wait_ge(s_diag, 2)
            e.reciprocal(bmv[:, 4:5], bmv[:, 3:4]).then_inc(s_ey, 1)
            e.wait_ge(s_ey, len(ECH) + 3)
            e.tensor_tensor(bmv[:, 5:6], bmv[:, 4:5], cols[:, 2:3], ALU.mult).then_inc(s_ey, 1)
            e.wait_ge(s_ey, len(ECH) + 4)
            e.tensor_tensor(bmv[:, 6:7], bmv[:, 0:1], bmv[:, 5:6], ALU.mult).then_inc(s_ey, 1)
            e.tensor_scalar(diag[0:F, :], ident[0:F, 0:F], bmv[:, 5:6], None, ALU.mult)
            e.wait_ge(s_ey, len(ECH) + 5)
            e.tensor_tensor(bmv[:, 7:8], cols[:, 3:4], bmv[:, 6:7], ALU.subtract).then_inc(s_ey, 1)
            e.wait_ge(s_xre, 32)
            for n, t0 in enumerate(range(0, NT, 8)):
                k = min(8, NT - t0)
                e.wait_ge(s_o, n + 1)
                e.tensor_tensor(xo[:, t0:t0 + k, :], xo[:, t0:t0 + k, :],
                                zps[:, n % NZB, 0:k * F].rearrange("p (t f) -> p t f", f=F), ALU.add).then_inc(s_oc, 1)

        @block.tensor
        def _(e):
            e.wait_ge(s_cst, 5)
            e.wait_ge(s_small, 16 * 7)

            def transpose(to, frm, k):
                return e.matmul(to, lhsT=frm, rhs=ident[0:k, 0:k], is_transpose=True, start=True, stop=True)

            def bank(job):
                if at[job] >= NZB:
                    e.wait_ge(*nth[jobs[at[job] - NZB]])
                return bank_of(job)

            transpose(bank(("comp",))[0:R, 0:R], comp_sb[:, :], R).then_inc(s_pz, 1)
            transpose(bank(("resw",))[:, 0:F], resw_sb[:, :], F).then_inc(s_pz, 1)
            e.wait_ge(s_basis, 16)
            e.wait_ge(s_ez, 1)
            for n in range(F // CLS):
                b = bank(("w", n))
                for o in range(CLS):
                    for h in range(2):
                        last = e.matmul(b[h * F:(h + 1) * F, o * R:(o + 1) * R], lhsT=basis_sb[:, :, n * CLS + o],
                                        rhs=compT[:, :], start=True, stop=True)
                last.then_inc(s_pz, 1)

            def transposed_x(c):
                b = bank(("x", c))
                t0, t1 = c * BANK // P, min((c + 1) * BANK // P, NT)
                e.wait_ge(s_dup, c + 1)
                for t in range(t0, t1):
                    last = transpose(b[:, (t - t0) * P:(t - t0 + 1) * P],
                                     xdup[:, c % 2, t - t0, :, :].rearrange("p a f -> p (a f)"), P)
                last.then_inc(s_pz, 1)

            def three_parts(to, stationary, moving):
                for a, (px, pw) in enumerate(((0, 0), (0, 1), (1, 2))):
                    last = e.matmul(to, lhsT=stationary(px, pw), rhs=moving(px, pw), start=(a == 0), stop=(a == 2))
                return last

            def product(c, t):
                b = bank(("z", c, t))
                ch, n0 = divmod(t * P, BANK)
                if c == 0 and n0 == 0:
                    e.wait_ge(s_xo, ch + 1)
                    e.wait_ge(s_p2, X0 + ch + 1)
                three_parts(b, lambda px, pw: xp[:, ch, px, n0:n0 + P],
                            lambda px, pw: wp[:, pw, c * CLS:(c + 1) * CLS, :].rearrange("p r f -> p (r f)")).then_inc(s_pz, 1)

            for c in range(NCH + AHEAD):
                if c < NCH:
                    transposed_x(c)
                if c >= AHEAD:
                    for t in range((c - AHEAD) * 4, min((c - AHEAD + 1) * 4, NT)):
                        product(0, t)

            def edges(ch, g, frm, s_free, n, s_to):
                if n:
                    e.wait_ge(s_free, n)
                for i in range(GT):
                    last = transpose(mflat[:, i * P:i * P + g], frm[0:g, ch, i * P:(i + 1) * P], g)
                last.then_inc(s_to, 1)

            e.wait_ge(s_wgt, 16 * 4)
            n = 0
            for ch, g in ((0, GA), (1, GB)):
                e.wait_ge(s_met, ch + 1)
                for frm in (idx_f, rel_f, wgt_f):
                    edges(ch, g, frm, s_me, n, s_mt)
                    n += 1
            e.wait_ge(s_me, 6)
            for k, b in ((0, 0), (2, 1)):
                transpose(mps[0:1, b, 0:GA], gstat[:, 0, k:k + 1], GA)
                last = transpose(mps[0:1, b, GA:NG], gstat[0:GB, 1, k:k + 1], GB)
            last.then_inc(s_mt, 1)

            for c in range(1, NCLS):
                for t in range(NT):
                    product(c, t)
            for c in range(NCH):
                b = bank(("r", c))
                w = min(BANK, NT * P - c * BANK)
                three_parts(b[0:F, 0:w], lambda px, pw: wp[:, pw, R, :], lambda px, pw: xp[:, c, px, 0:w]).then_inc(s_pz, 1)

            flag = fast_path_flag(e)
            with e.If(flag < 1):
                e.wait_ge(s_g["dst"], 1)
                edges(0, GA, rel_f, s_g["me"], 0, s_g["mt"])
                edges(1, GB, rel_f, s_g["me"], 1, s_g["mt"])
                e.wait_ge(s_g["me"], 2)
                with e.Fori(0, NTILES) as t:
                    e.wait_ge(s_g["bcast"], t + 1)
                    transpose(mps[:, 0, 0:P], gdstb[:, :], P).then_inc(s_g["row"], 1)
                    e.wait_ge(s_g["tc"], t + 1)
                    e.matmul(mps[:, 1, 0:F], lhsT=geq[:, :], rhs=gyn[:, :], start=True, stop=True).then_inc(s_g["mm"], 1)
                e.wait_ge(s_g["back"], 16)
                for q in range(NQ):
                    if q >= 2:
                        e.wait_ge(s_g["back"], 16 + q - 1)
                    transpose(aps[:, q % 2, 0:P], xo[:, 2 * q:2 * q + 2, :].rearrange("p t f -> p (t f)"), P).then_inc(s_g["tp"], 1)
            with e.Else():
                for t in range(NTILES):
                    g, i = divmod(t, GT)
                    if i == 0 and g >= 2:
                        e.wait_ge(s_acc, g)
                    e.wait_ge(s_y[t % NY], 16 * (t // NY + 1))
                    e.wait_ge(s_oh, t + 1)
                    h = (i % 2) * F
                    e.matmul(aps[h:h + F, g % 2, 0:WIN], lhsT=ys[:, t % NY, :], rhs=oh[:, t % NOH, :],
                             start=(i < 2), stop=(i >= GT - 2 or t >= NTILES - 2)).then_inc(s_agg, 1)

            e.wait_ge(s_sum, 1)
            for n, (c0, w) in enumerate(ECH):
                if n >= 2:
                    e.wait_ge(s_eh, n - 1)
                e.matmul(aps[0:F, n % 2, 0:w], lhsT=stack2[:, :], rhs=acc[:, c0:c0 + w], start=True, stop=True).then_inc(s_e1, 1)
            e.wait_ge(s_ey, len(ECH) + 6)
            e.matmul(mps[F:F + 1, 0, 0:F], lhsT=bmv[:, 7:8], rhs=ident[0:F, 0:F], start=True, stop=True).then_inc(s_sh, 1)
            e.wait_ge(s_shc, 1)
            for n, t0 in enumerate(range(0, NT, 8)):
                if n >= NZB:
                    e.wait_ge(s_oc, n - NZB + 1)
                for t in range(t0, min(t0 + 8, NT)):
                    last = e.matmul(zps[:, n % NZB, (t - t0) * F:(t - t0 + 1) * F], lhsT=acc[0:F + 1, t * P:(t + 1) * P],
                                    rhs=diag[:, :], start=True, stop=True)
                last.then_inc(s_o, 1)


_INS = ["x", "src", "dst", "edge_type_64", "edge_weight1", "L0_gnn_basis", "L0_gnn_comp", "L0_gnn_bias",
        "L0_gnn_res_w", "L0_gnn_res_b", "L0_gnn_gamma", "L0_gnn_beta"]


def kernel(**inputs):
    import numpy as np
    import concourse.bacc as bacc
    from concourse.bass_utils import run_bass_kernel_spmd

    nc = bacc.Bacc("TRN2", target_bir_lowering=False, num_devices=1)
    arrays, args = {}, []
    for name in _INS:
        a = np.ascontiguousarray(inputs[name])
        if name == "edge_weight1":
            a = a.reshape(-1)
        arrays[f"in_{name}"] = a
        args.append(nc.dram_tensor(f"in_{name}", a.shape, mybir.dt.from_np(a.dtype), kind="ExternalInput").ap())
    shape = inputs["x"].shape
    args.append(nc.dram_tensor("out_x", shape, F32, kind="ExternalOutput").ap())
    rgcn_kernel(nc, *args)
    r = run_bass_kernel_spmd(nc, [arrays], core_ids=[0])
    return r.results[0]["out_x"]
```

```python
import math
from contextlib import ExitStack

import concourse.bass as bass
from concourse import mybir

F32 = mybir.dt.float32
I32 = mybir.dt.int32
BF16 = mybir.dt.bfloat16
ALU = mybir.AluOpType
ACT = mybir.ActivationFunctionType
AX = mybir.AxisListType.X

P = 128
BANK = 512
LN_EPS = 1e-5
BN_EPS = 1e-5
GT = 8
GE = GT * P
WIN = 192
CLS = 8
NZB = 4
ZT = 4
NZS = 4
NY = 16
NOH = 8
LNT = 14
EARLY = {0: (3, 2), 64: (4, 3), 128: (6, 5)}
DONE_GROUP, DONE_NODES, DONE_STEP = 176, 9216, 5
LANDING_US, GATHER_US, SUM_US, PRODUCT_US = 12.0, 1.04, 0.2, 0.7


def rgcn_kernel(nc, x, src, dst, etype, weight, basis, comp, bias, res_w, res_b, gamma, beta, out):
    N, F = x.shape
    E = src.shape[0]
    R = comp.shape[0]
    NT = math.ceil(N / P)
    LAST = N - (NT - 1) * P
    NQ = NT // 2
    NCH = math.ceil(NT * P / BANK)
    NCLS = R // CLS
    NG = math.ceil(E / GE)
    LE = E - (NG - 1) * GE
    NTILES = math.ceil(E / P)
    GA, GB = P, NG - P
    NLN = NT // LNT
    TAKE_FROM = 2
    assert NLN + 2 == F // CLS + 1 and NT % 2 == 0 and NT % LNT == 0 and CLS * F == BANK and 64 < GB <= P and F == 64 and R == 64
    early = [EARLY[max(first for first in EARLY if first <= g)] for g in range(NG - 1)]
    units = [(g, range(tiles), classes) for g, (classes, tiles) in enumerate(early)]
    units += [(g, range(tiles, GT), NCLS) for g, (_, tiles) in enumerate(early)]
    units += [(NG - 1, range(NTILES - (NG - 1) * GT), NCLS)]
    seq = [(g * GT + i, u, k, len(tiles), classes) for u, (g, tiles, classes) in enumerate(units) for k, i in enumerate(tiles)]
    FIRST_CLS = early[0][0]
    METAS = [("idx", 0, GA), ("rel", 0, GA), ("wgt", 0, GA), ("stats",), ("idx", 1, GB), ("rel", 1, GB), ("wgt", 1, GB)]
    METAS_AT = [(FIRST_CLS - 1, t) for t in (22, 30, 38, 46, NT - 18, NT - 12, NT - 6)]
    LEAD = 4
    SOURCES_AT, TYPES_AT, ROWS_AT = [1, 2], [6, 8], [11, 12]
    SORT_STAGES = int(math.log2(GE))
    assert N * GE <= 1 << 24
    unit_end = [n for n, (_, _, k, size, _) in enumerate(seq) if k == size - 1]
    assert len(seq) == NTILES
    EPI = 2 * BANK
    NEPI = math.ceil(NT * P / EPI)
    EPI_EARLY = DONE_NODES // EPI
    epi_width = [min(BANK, NT * P // 2 - n * BANK) for n in range(NEPI)]
    done_unit = max(u for u, (g, _, _) in enumerate(units) if g < DONE_GROUP)
    epi_after = [unit_end[done_unit] + (n + 1) * DONE_STEP for n in range(EPI_EARLY)]
    assert DONE_NODES % EPI == 0 and epi_after[-1] + NOH + 1 < NTILES
    DUMP = NT * P
    ROWS = DUMP + P

    table = nc.dram_tensor("z_table", [NCLS * N * CLS, F], F32)
    accd = nc.dram_tensor("acc_rows", [ROWS, F], F32)

    with ExitStack() as ctx:
        def sb(name, shape, dt=F32):
            return ctx.enter_context(nc.sbuf_tensor(name, shape, dt))

        def sem(name):
            return ctx.enter_context(nc.semaphore(name))

        ARENA = NT * P + WIN + 16
        acc = sb("acc", [P, ARENA])
        ar_f = acc[:, 0:6 * 2 * GE].rearrange("p (a c n) -> p a c n", a=6, c=2)
        ar_i = acc[:, 0:6 * 2 * GE].bitcast(I32).rearrange("p (a c n) -> p a c n", a=6, c=2)
        dst_i, src_i, ety_i, key_i = (ar_i[:, k] for k in range(4))
        dst_f, late_f, cnt_f, key_f, idx_f, wgt_f = (ar_f[:, k] for k in range(6))
        rel_f, idx_i = key_f, ar_i[:, 4]
        res = sb("res", [P, NCH, BANK])
        xp = res[:, :, :].bitcast(BF16).rearrange("p c (a n) -> p c a n", a=2)
        basis_sb = res[0:R, 0:F * F // BANK, :].rearrange("b q n -> b (q n)").rearrange("b (i o) -> b i o", o=F)
        xr = res[:, :, :].rearrange("p c n -> p (c n)")[:, NCH * BANK - NT * F:].rearrange("p (t f) -> p t f", f=F)
        wp = sb("wp", [P, 3, R + 1, F], BF16)
        shared = sb("shared", [P, 2 * LNT * F + 4 * BANK])
        xdup = shared[:, 0:2 * BANK].rearrange("p (s t a f) -> p s t a f", s=2, a=2, f=F)
        rem = shared[:, 2 * BANK:4 * BANK].rearrange("p (s n) -> p s n", s=2)
        sq = shared[:, 4 * BANK:4 * BANK + 2 * LNT * F].rearrange("p (s t f) -> p s t f", s=2, f=F)
        ys = shared[:, 0:NY * F].rearrange("p (s f) -> p s f", f=F)
        oh = shared[:, NY * F:NY * F + NOH * WIN].rearrange("p (s n) -> p s n", n=WIN)
        gdstb, geq, gjunk = (shared[:, k * P:(k + 1) * P] for k in range(3))
        x2l = sb("x2l", [F, BANK], BF16)
        zst = sb("zst", [P, NZS, ZT, BANK])
        zflat = zst[:, :, :, :].rearrange("p s t n -> p (s t n)")
        xo = zflat[:, 0:NT * F].rearrange("p (t f) -> p t f", f=F)
        mom = sb("mom", [P, 4, NT])
        idx_all = sb("idx_all", [P, NG * GT], I32)
        rel_all = sb("rel_all", [P, NG * GT])
        wgt_all = sb("wgt_all", [P, NG * GT])
        ident = sb("ident", [P, P])
        stack2 = sb("stack2", [P, F])
        ones = sb("ones", [P, P])
        lower = sb("lower", [P, P])
        iota = sb("iota", [P, WIN])
        dumprow = sb("dumprow", [P, 1])
        place = sb("place", [P, GE])
        smask = sb("smask", [P, GE // 2], I32)
        late_from = sb("late_from", [P, 2])
        count_to_span = sb("count_to_span", [P, 2])
        comp_sb = sb("comp_sb", [R, R])
        compT = sb("compT", [R, R])
        resw_sb = sb("resw_sb", [F, 2 * F])
        cols = sb("cols", [P, 4])
        gstat = sb("gstat", [P, 2, 3])
        base_i = sb("base_i", [1, NG], I32)
        span_r = sb("span_r", [1, NG])
        flag_f = sb("flag_f", [1, 2])
        flag_i = sb("flag_i", [1, 1], I32)
        bst = sb("bst", [P, NEPI, 6])
        halves = sb("halves", [P, 2])
        bmv = sb("bmv", [P, 10])
        wmean = sb("wmean", [P, P])
        wdiff = sb("wdiff", [P, P])
        gdst = sb("gdst", [P, 2])
        gnum = sb("gnum", [P, 4])
        gidx = sb("gidx", [P, 1], I32)
        gsidx = sb("gsidx", [P, 1], I32)
        gy = sb("gy", [P, F])
        gyn = sb("gyn", [P, F])
        gsum = sb("gsum", [P, F])

        zps = ctx.enter_context(nc.psum_tensor("zps", [P, NZB, BANK], F32))
        aps = ctx.enter_context(nc.psum_tensor("aps", [P, 2, BANK], F32))
        mps = ctx.enter_context(nc.psum_tensor("mps", [P, 2, BANK], F32))
        mflat = mps[:, :, :].rearrange("p b n -> p (b n)")

        s_x = [sem(f"s_x{c}") for c in range(NLN)]
        s_small, s_basis = sem("s_small"), sem("s_basis")
        s_dst, s_idx, s_wgt = sem("s_dst"), sem("s_idx"), sem("s_wgt")
        s_pad = sem("s_pad")
        s_cst, s_pc = sem("s_cst"), sem("s_pc")
        s_xc, s_sq, s_var, s_dev, s_ln = (sem(n) for n in ("s_xc", "s_sq", "s_var", "s_dev", "s_ln"))
        s_pz, s_ez, s_ed = sem("s_pz"), sem("s_ez"), sem("s_ed")
        s_p1, s_rem, s_p2 = sem("s_p1"), sem("s_rem"), sem("s_p2")
        s_dup = sem("s_dup")
        s_xo, s_xre = sem("s_xo"), sem("s_xre")
        s_zst = [sem(f"s_zst{k}") for k in range(NZS)]
        s_met, s_mt, s_me = sem("s_met"), sem("s_mt"), sem("s_me")
        s_flag = sem("s_flag")
        s_y = [sem(f"s_y{k}") for k in range(NY)]
        s_oh, s_agg, s_acc = sem("s_oh"), sem("s_agg"), sem("s_acc")
        s_dv = sem("s_dv")
        s_sum = sem("s_sum")
        s_g = {k: sem(f"s_g_{k}") for k in
               ("dst", "mt", "me", "zero", "clr", "bcast", "row", "idx", "y", "mul", "mm", "sum", "add", "back", "tp", "tc", "go")}
        s_e1, s_eh, s_ey, s_bst, s_st, s_sc, s_o, s_oc, s_out = (
            sem(n) for n in ("s_e1", "s_eh", "s_ey", "s_bst", "s_st", "s_sc", "s_o", "s_oc", "s_out"))
        s_cols = sem("s_cols")
        s_src, s_cls, s_row = (sem(n) for n in ("s_src", "s_cls", "s_row"))

        AHEAD = 2
        jobs = [("comp",), ("resw",)] + [("w", n) for n in range(F // CLS)]
        for c in range(NCH + AHEAD):
            jobs += [("x", c)] if c < NCH else []
            jobs += [("z", 0, t) for t in range((c - AHEAD) * 4, min((c - AHEAD + 1) * 4, NT)) if c >= AHEAD]
        jobs += [("z", c, t) for c in range(1, NCLS) for t in range(NT)]
        jobs += [("r", n) for n in range(NEPI)]
        at = {job: n for n, job in enumerate(jobs)}
        nth = {}
        emptied = {s_ez: 0, s_ed: 0}
        for job in jobs:
            by = s_ez if job[0] in ("comp", "z", "r") else s_ed
            emptied[by] += 1
            nth[job] = (by, emptied[by])
        splits = [job for job in jobs if nth[job][0] is s_ed]
        X0 = splits.index(("x", 0))

        order, steps = [], 0
        for n in range(len(splits)):
            wanted = 4 if n >= 3 else n + 1
            if n >= X0:
                wanted = math.ceil(min((n - X0 + LEAD) * BANK // P, NT) / LNT) + 2
            while steps < min(wanted, NLN + 2):
                order.append(("norm", steps))
                steps += 1
            order.append(("split", n))
            if n - X0 in TYPES_AT:
                order.append(("types", TYPES_AT.index(n - X0)))
        act_order = [item for item in order if item[0] != "types"]
        for n in range(len(act_order) - 2, 0, -1):
            before, this, after = (act_order[n + d] for d in (-1, 0, 1))
            if this[0] == "norm" and before[0] == after[0] == "split" and after[1] > X0:
                act_order[n:n + 2] = [after, this]

        def bank_of(job):
            return zps[:, at[job] % NZB, :]

        ZG = [(t, min(ZT, NT - 1 - t)) for t in range(0, NT - 1, ZT)] + [(NT - 1, 1)]
        STORES = [(c, t0, k) for c in range(NCLS) for t0, k in ZG]
        zview = table[:, :].rearrange("(c n r) f -> c n (r f)", c=NCLS, r=CLS)

        def evac_done_of_store(n):
            return 1 + sum(k for _, _, k in STORES[:n + 1])

        def table_landed(e, classes):
            for k in range(NZS):
                e.wait_ge(s_zst[k], 16 * len(range(k, classes * len(ZG), NZS)))

        def fast_path_flag(e):
            e.wait_ge(s_flag, 1)
            return e.value_load(flag_i[0:1, 0:1], min_val=0, max_val=1)

        block = ctx.enter_context(nc.Block())

        @block.sync
        def _(e):
            xv = x[0:(NT - 1) * P, :].rearrange("(t p) f -> p t f", p=P)
            for c in range(NLN):
                t0, t1 = c * LNT, min((c + 1) * LNT, NT - 1)
                e.dma_start(xr[:, t0:t1, :], xv[:, t0:t1, :]).then_inc(s_x[c], 16)
            e.wait_ge(s_pad, 1)
            e.dma_start(xr[0:LAST, NT - 1, :], x[(NT - 1) * P:N, :]).then_inc(s_x[NLN - 1], 16)
            e.wait_ge(s_pad, 2)
            for arr, to, s in ((dst, dst_i, s_dst), (src, src_i, s_idx), (etype, ety_i, s_idx), (weight, wgt_f, s_wgt)):
                e.dma_start(to[:, 0, :], arr[0:P * GE].rearrange("(g n) -> g n", n=GE)).then_inc(s, 16)
                e.dma_start(to[0:64, 1, :], arr[P * GE:(P + 64) * GE].rearrange("(g n) -> g n", n=GE)).then_inc(s, 16)
                e.dma_start(to[64:GB - 1, 1, :], arr[(P + 64) * GE:(NG - 1) * GE].rearrange("(g n) -> g n", n=GE)).then_inc(s, 16)
                e.dma_start(to[GB - 1:GB, 1, 0:LE], arr[E - LE:E].rearrange("(g n) -> g n", n=LE)).then_inc(s, 16)
                if arr is not weight:
                    e.dma_start(to[GB - 1:GB, 1, LE:GE], arr[E - (GE - LE):E].rearrange("(g n) -> g n", n=GE - LE)).then_inc(s, 16)
            for n, (c, t0, k) in enumerate(STORES):
                e.wait_ge(s_ez, evac_done_of_store(n))
                rows = LAST if t0 == NT - 1 else P
                e.dma_start(zview[c, t0 * P:t0 * P + (k - 1) * P + rows, :].rearrange("(t p) w -> p t w", p=rows),
                            zst[0:rows, n % NZS, 0:k, :]).then_inc(s_zst[n % NZS], 16)
            flag = fast_path_flag(e)
            with e.If(flag < 1):
                e.wait_ge(s_g["zero"], 1)
                av = accd[:, :].rearrange("(p t) f -> p (t f)", p=P)
                width = ROWS // P * F
                cuts = list(range(0, width, 2048)) + [width]
                for a, b in zip(cuts, cuts[1:]):
                    e.dma_start(av[:, a:b], zflat[:, 0:b - a]).then_inc(s_g["clr"], 16)
                e.wait_ge(s_g["add"], 16 * NTILES)
                e.wait_ge(s_g["clr"], 16 * (len(cuts) - 1))
                e.dma_start(xo, accd[0:NT * P, :].rearrange("(t p) f -> p t f", p=P)).then_inc(s_g["back"], 16)
                e.wait_ge(s_sum, 1)
            table_landed(e, NCLS)
            e.dma_start(xo[:, 0:NT - 1, :], xv).then_inc(s_xre, 16)
            e.dma_start(xo[0:LAST, NT - 1, :], x[(NT - 1) * P:N, :]).then_inc(s_xre, 16)
            ov = out[0:(NT - 1) * P, :].rearrange("(t p) f -> p t f", p=P)
            for n, t0 in enumerate(range(0, NT, 8)):
                t1 = min(t0 + 8, NT - 1)
                e.wait_ge(s_oc, n + 1)
                e.dma_start(ov[:, t0:t1, :], xo[:, t0:t1, :]).then_inc(s_out, 16)
            e.dma_start(out[(NT - 1) * P:N, :], xo[0:LAST, NT - 1, :]).then_inc(s_out, 16)
            e.wait_ge(s_out, 16 * (math.ceil(NT / 8) + 1))

        @block.gpsimd
        def _(e):
            e.memset(ident[:, :], 0.0).then_inc(s_pc, 1)
            e.memset(stack2[:, :], 0.0).then_inc(s_pc, 1)
            e.memset(lower[:, :], 0.0).then_inc(s_pc, 1)
            e.memset(ones[:, :], 1.0)
            e.wait_ge(s_pc, 3)
            e.affine_select(out=ident[:, :], in_=ident[:, :], compare_op=ALU.not_equal, fill=1.0,
                            base=0, pattern=[[-1, P]], channel_multiplier=1).then_inc(s_cst, 1)
            e.affine_select(out=lower[:, :], in_=lower[:, :], compare_op=ALU.is_ge, fill=1.0,
                            base=0, pattern=[[1, P]], channel_multiplier=-1).then_inc(s_cst, 1)
            e.affine_select(out=stack2[:, :], in_=stack2[:, :], compare_op=ALU.not_equal, fill=1.0,
                            base=0, pattern=[[-1, F]], channel_multiplier=1).then_inc(s_pc, 1)
            e.wait_ge(s_pc, 4)
            e.affine_select(out=stack2[:, :], in_=stack2[:, :], compare_op=ALU.not_equal, fill=1.0,
                            base=-F, pattern=[[-1, F]], channel_multiplier=1).then_inc(s_cst, 1)
            e.iota(iota[:, :], [[1, WIN]], base=0, channel_multiplier=0,
                   allow_small_or_imprecise_dtypes=True).then_inc(s_cst, 1)
            e.iota(dumprow[:, :], [[1, 1]], base=DUMP, channel_multiplier=1,
                   allow_small_or_imprecise_dtypes=True).then_inc(s_cst, 1)
            e.iota(place[:, :], [[-1, GE]], base=0, channel_multiplier=0, allow_small_or_imprecise_dtypes=True)
            assert set(EARLY) == {0, 64, P}
            e.memset(late_from[:, 0:1], float(early[64][0] * CLS)).then_inc(s_pc, 1)
            e.memset(late_from[:, 1:2], float(early[P][0] * CLS)).then_inc(s_pc, 1)
            e.memset(count_to_span[:, 0:1], float(WIN - 1 - (GE - early[64][1] * P))).then_inc(s_pc, 1)
            e.memset(count_to_span[:, 1:2], float(WIN - 1 - (GE - early[P][1] * P)))
            e.wait_ge(s_pc, 7)
            e.memset(late_from[0:64, 0:1], float(early[0][0] * CLS))
            e.memset(count_to_span[0:64, 0:1], float(WIN - 1 - (GE - early[0][1] * P)))
            e.affine_select(out=late_from[:, 1:2], in_=late_from[:, 1:2], compare_op=ALU.not_equal, fill=float(R),
                            base=-(GB - 1), pattern=[[0, 1]], channel_multiplier=1).then_inc(s_cst, 1)
            for c in range(NCH):
                t0, t1 = c * BANK // P, min((c + 1) * BANK // P, NT)
                e.wait_ge(s_ln, math.ceil(t1 / LNT))
                if c >= 2:
                    e.wait_ge(s_pz, at["x", c - 2] + 1)
                for k in range(2):
                    last = e.tensor_tensor(xdup[:, c % 2, 0:t1 - t0, k, :], xr[:, t0:t1, :],
                                           mom[:, 3, t0:t1].unsqueeze(2).broadcast_to([P, t1 - t0, F]), ALU.mult)
                last.then_inc(s_dup, 1)
                if c in SOURCES_AT + ROWS_AT:
                    ch = (c in SOURCES_AT[1:]) + (c in ROWS_AT[1:])
                    g = (GA, GB)[ch]
                    sources, idx = late_f[0:g, ch, :], idx_f[0:g, ch, :]
                    if c in SOURCES_AT:
                        e.wait_ge(s_idx, 16 * 10)
                        e.tensor_scalar(sources, src_i[0:g, ch, :], float(CLS), None, ALU.mult).then_inc(s_src, 1)
                    else:
                        e.wait_ge(s_cls, ch + 1)
                        e.wait_ge(s_src, ch + 1)
                        e.tensor_tensor(idx, idx, sources, ALU.add).then_inc(s_row, 1)
            table_landed(e, FIRST_CLS)
            flag = fast_path_flag(e)
            with e.If(flag < 1):
                table_landed(e, NCLS)
                e.wait_ge(s_me, len(METAS))
                e.wait_ge(s_g["clr"], 16 * math.ceil(ROWS // P * F / 2048))
                with e.Fori(0, NTILES) as t:
                    e.tensor_copy(gidx[:, :], idx_all[:, bass.ds(t, 1)]).then_inc(s_g["idx"], 1)
                    e.wait_ge(s_g["idx"], t + 1)
                    e.sem_inc(s_g["go"], 1)
                    e.indirect_dma_start(out=gy[:, :], out_offset=None, in_=table[:, :],
                                         in_offset=bass.IndirectOffsetOnAxis(ap=gidx[:, :], axis=0)).then_inc(s_g["y"], 16)
                    e.wait_ge(s_g["sum"], t + 1)
                    e.sem_inc(s_g["go"], 1)
                    e.indirect_dma_start(out=accd[:, :], out_offset=bass.IndirectOffsetOnAxis(ap=gsidx[:, :], axis=0),
                                         in_=gsum[:, :], in_offset=None, compute_op=ALU.add).then_inc(s_g["add"], 16)
                    e.wait_ge(s_g["add"], t * 16 + 16)
            with e.Else():
                for t, (col, _, _, _, classes) in enumerate(seq):
                    if t and classes != seq[t - 1][4]:
                        table_landed(e, classes)
                    if col == GA * GT:
                        e.wait_ge(s_me, len(METAS))
                    if t >= NY:
                        e.wait_ge(s_agg, t - NY + 1)
                    e.indirect_dma_start(out=ys[:, t % NY, :], out_offset=None, in_=table[0:classes * N * CLS, :],
                                         in_offset=bass.IndirectOffsetOnAxis(ap=idx_all[:, col:col + 1], axis=0)
                                         ).then_inc(s_y[t % NY], 16)

        @block.scalar
        def _(e):
            e.dma_start(comp_sb[:, :], comp).then_inc(s_small, 16)
            e.dma_start(resw_sb[:, 0:F], res_w).then_inc(s_small, 16)
            e.dma_start(resw_sb[:, F:2 * F], res_w).then_inc(s_small, 16)
            e.dma_start(basis_sb, basis).then_inc(s_basis, 16)
            for k, v in enumerate((bias, res_b, gamma, beta)):
                for h in range(2):
                    e.dma_start(cols[h * F:(h + 1) * F, k:k + 1], v.rearrange("(f a) -> f a", a=1)).then_inc(s_cols, 16)

            def take(job, to, frm):
                e.wait_ge(s_pz, at[job] + 1)
                e.activation(to, frm, ACT.Copy).then_inc(s_ez, 1)

            def square(c):
                e.wait_ge(s_xc, c + 1)
                if c >= 2:
                    e.wait_ge(s_var, c - 1)
                e.activation(sq[:, c % 2, :, :], xr[:, c * LNT:(c + 1) * LNT, :], ACT.Square).then_inc(s_sq, 1)

            def deviation(c):
                e.wait_ge(s_var, c + 1)
                e.activation(mom[:, 3, c * LNT:(c + 1) * LNT], mom[:, 2, c * LNT:(c + 1) * LNT], ACT.Sqrt).then_inc(s_dev, 1)

            def first_part(n):
                kind, *c = splits[n]
                b = bank_of(splits[n])
                e.wait_ge(s_pz, at[splits[n]] + 1)
                if kind == "resw":
                    to, frm = wp[:, 0, R, :], b[:, 0:F]
                elif kind == "w":
                    to, frm = wp[:, 0, 0:R, c[0] * CLS:(c[0] + 1) * CLS], b.rearrange("p (o r) -> p r o", r=R)
                else:
                    w = min(BANK, NT * P - c[0] * BANK)
                    to, frm = xp[:, c[0], 1, 0:w], b[:, 0:w]
                if kind == "w":
                    e.activation(wp[0:F, 2, 0:R, c[0] * CLS:(c[0] + 1) * CLS], frm[0:F], ACT.Copy)
                e.activation(to, frm, ACT.Relu if kind == "x" else ACT.Copy).then_inc(s_p1, 1)

            def second_part(c):
                n = X0 + c
                w = min(BANK, NT * P - c * BANK)
                e.wait_ge(s_rem, n + 1)
                e.activation(xp[F:P, c, 0, 0:w], rem[F:P, n % 2, 0:w], ACT.Copy).then_inc(s_p2, 1)

            def products(n):
                c, t0, k = STORES[n]
                rows = LAST if t0 == NT - 1 else P
                if n >= NZS:
                    e.wait_ge(s_zst[n % NZS], 16 * (n // NZS))
                for i in range(k):
                    take(("z", c, t0 + i), zst[0:rows, n % NZS, i, :], bank_of(("z", c, t0 + i))[0:rows, :])

            take(("comp",), compT[:, :], bank_of(("comp",))[0:R, 0:R])
            for kind, n in act_order:
                if kind == "norm":
                    if n < NLN:
                        square(n)
                    if 1 <= n <= NLN:
                        deviation(n - 1)
                elif kind == "split":
                    first_part(n)
                    c = n - X0
                    if c >= 1:
                        second_part(c - 1)
                    if c >= 2:
                        products(c - 2)
            second_part(NCH - 1)
            products(NCH - 2)
            products(NCH - 1)
            for n in range(NCH, len(STORES)):
                products(n)
            e.wait_ge(s_cols, 16 * 8)
            for n in range(NEPI):
                w = epi_width[n]
                e.wait_ge(s_pz, at["r", n] + 1)
                e.activation(res[:, 2 * n, 0:w], bank_of(("r", n))[:, 0:w], ACT.Relu, bias=cols[:, 1:2]).then_inc(s_ez, 1)

            for n, w in enumerate(epi_width):
                e.wait_ge(s_e1, n + 1)
                e.activation(acc[:, n * EPI:n * EPI + w], zps[:, n % NZB, 0:w], ACT.Relu, bias=cols[:, 0:1]).then_inc(s_eh, 1)
            e.wait_ge(s_st, 4)
            e.activation(bmv[:, 4:5], bmv[:, 3:4], ACT.Sqrt).then_inc(s_st, 1)
            e.wait_ge(s_st, 9)
            for n, w in enumerate(epi_width):
                y = acc[:, n * EPI:n * EPI + w]
                e.activation(y, y, ACT.Identity, scale=bmv[:, 6:7], bias=bmv[:, 8:9]).then_inc(s_sc, 1)

        @block.vector
        def _(e):
            steps = [0]

            def link(ins):
                steps[0] += 1
                ins.then_inc(s_dv, 1)
                e.wait_ge(s_dv, steps[0])

            e.memset(xr[:, NT - 1, :], 0.0).then_inc(s_pad, 1)
            e.memset(wgt_f[64:GB, 1, :], 0.0).then_inc(s_pad, 1)
            def centre(c):
                t0, t1 = c * LNT, (c + 1) * LNT
                e.wait_ge(s_x[c], 32 if c == NLN - 1 else 16)
                link(e.tensor_reduce(mom[:, 0, t0:t1], xr[:, t0:t1, :], AX, ALU.add))
                link(e.tensor_scalar(mom[:, 1, t0:t1], mom[:, 0, t0:t1], 1.0 / F, None, ALU.mult))
                e.tensor_tensor(xr[:, t0:t1, :], xr[:, t0:t1, :],
                                mom[:, 1, t0:t1].unsqueeze(2).broadcast_to([P, LNT, F]), ALU.subtract).then_inc(s_xc, 1)

            def variance(c):
                t0, t1 = c * LNT, (c + 1) * LNT
                e.wait_ge(s_sq, c + 1)
                link(e.tensor_reduce(mom[:, 2, t0:t1], sq[:, c % 2, :, :], AX, ALU.add))
                e.tensor_scalar(mom[:, 2, t0:t1], mom[:, 2, t0:t1], 1.0 / F, LN_EPS, ALU.mult, ALU.add).then_inc(s_var, 1)

            def scale(c):
                t0, t1 = c * LNT, (c + 1) * LNT
                e.wait_ge(s_dev, c + 1)
                e.reciprocal(mom[:, 3, t0:t1], mom[:, 3, t0:t1]).then_inc(s_ln, 1)

            def split(n):
                kind, *c = splits[n]
                b = bank_of(splits[n])
                if n >= 2:
                    e.wait_ge(s_p2, n - 1)
                e.wait_ge(s_p1, n + 1)
                if kind != "x":
                    if kind == "resw":
                        k, o0, o1, frm = slice(R, R + 1), 0, F, b[:, 0:F].unsqueeze(1)
                        r_all = rem[:, n % 2, 0:F].unsqueeze(1)
                    else:
                        k, o0, o1 = slice(0, R), c[0] * CLS, (c[0] + 1) * CLS
                        frm = b.rearrange("p (o r) -> p r o", r=R)
                        r_all = rem[:, n % 2, :].rearrange("p (o r) -> p r o", r=R)
                    e.tensor_tensor(r_all, frm, wp[:, 0, k, o0:o1], ALU.subtract).then_inc(s_rem, 1)
                    if kind == "resw":
                        e.tensor_copy(wp[0:F, 2, k, o0:o1], wp[0:F, 0, k, o0:o1])
                    e.wait_ge(s_rem, n + 1)
                    link(e.tensor_copy(wp[:, 1, k, o0:o1], r_all))
                    e.tensor_tensor(wp[F:P, 2, k, o0:o1], r_all[F:P], wp[F:P, 1, k, o0:o1], ALU.subtract).then_inc(s_p2, 1)
                    e.sem_inc(s_ed, 1)
                else:
                    c = c[0]
                    w = min(BANK, NT * P - c * BANK)
                    e.scalar_tensor_tensor(out=rem[:, n % 2, 0:w], in0=b[:, 0:w], scalar=0.0, in1=xp[:, c, 1, 0:w],
                                           op0=ALU.max, op1=ALU.subtract).then_inc(s_rem, 1)
                    e.tensor_copy(xp[0:F, c, 0, 0:w], xp[0:F, c, 1, 0:w]).then_inc(s_ed, 1)
                    e.wait_ge(s_rem, n + 1)
                    link(e.tensor_copy(x2l[:, 0:w], rem[0:F, n % 2, 0:w]))
                    e.tensor_tensor(xp[0:F, c, 1, 0:w], rem[0:F, n % 2, 0:w], x2l[:, 0:w], ALU.subtract).then_inc(s_xo, 1)

            for kind, *n in order:
                if kind == "norm":
                    if n[0] < NLN:
                        centre(n[0])
                    if 1 <= n[0] <= NLN:
                        variance(n[0] - 1)
                    if n[0] >= 2:
                        scale(n[0] - 2)
                elif kind == "split":
                    split(n[0])
                else:
                    ch, g = n[0], (GA, GB)[n[0]]
                    e.wait_ge(s_idx, 16 * 10)
                    link(e.tensor_scalar(idx_i[0:g, ch, :], ety_i[0:g, ch, :], int(math.log2(CLS)), None,
                                         ALU.logical_shift_right))
                    e.scalar_tensor_tensor(out=idx_f[0:g, ch, :], in0=idx_i[0:g, ch, :], scalar=float(CLS * N - CLS),
                                           in1=ety_i[0:g, ch, :], op0=ALU.mult, op1=ALU.add).then_inc(s_cls, 1)

            e.wait_ge(s_dst, 16 * 5)
            e.wait_ge(s_cst, 6)
            link(e.tensor_scalar(place[:, :], place[:, :], 1.0 / GE, None, ALU.mult))
            def places(ch, g):
                e.tensor_reduce(gstat[0:g, ch, 0:1], dst_i[0:g, ch, :], AX, ALU.min)
                link(e.tensor_reduce(gstat[0:g, ch, 1:2], dst_i[0:g, ch, :], AX, ALU.max))
                e.tensor_scalar(dst_f[0:g, ch, :], dst_i[0:g, ch, :], gstat[0:g, ch, 0:1], None, ALU.subtract)
                e.tensor_tensor(gstat[0:g, ch, 2:3], gstat[0:g, ch, 1:2], gstat[0:g, ch, 0:1], ALU.subtract)
                e.wait_ge(s_row, ch + 1)
                link(e.tensor_scalar(late_f[0:g, ch, :], ety_i[0:g, ch, :], late_from[0:g, ch:ch + 1], None, ALU.is_ge))
                link(e.tensor_tensor_scan(cnt_f[0:g, ch, :], late_f[0:g, ch, :], late_f[0:g, ch, :], 0.0, ALU.add, ALU.bypass))
                e.tensor_scalar(gstat[0:g, ch, 2:3], cnt_f[0:g, ch, GE - 1:GE], count_to_span[0:g, ch:ch + 1],
                                gstat[0:g, ch, 2:3], ALU.add, ALU.max)
                link(e.scalar_tensor_tensor(out=key_f[0:g, ch, :], in0=place[0:g, :], scalar=1.0,
                                            in1=late_f[0:g, ch, :], op0=ALU.add, op1=ALU.mult))
                link(e.tensor_tensor(late_f[0:g, ch, :], key_f[0:g, ch, :], place[0:g, :], ALU.subtract))
                link(e.scalar_tensor_tensor(out=late_f[0:g, ch, :], in0=late_f[0:g, ch, :], scalar=float(GE),
                                            in1=cnt_f[0:g, ch, :], op0=ALU.mult, op1=ALU.subtract))
                link(e.scalar_tensor_tensor(out=key_i[0:g, ch, :], in0=dst_f[0:g, ch, :], scalar=float(GE),
                                            in1=late_f[0:g, ch, :], op0=ALU.mult, op1=ALU.add))

            def exchange(ch, g, k):
                pairs = ar_i[0:g, 3:6, ch, :].rearrange("p a (b h w) -> p a b h w", h=2, w=1 << k)
                first, second = pairs[:, :, :, 0, :], pairs[:, :, :, 1, :]
                kept = ar_i[0:g, 0:3, ch, 0:GE // 2].rearrange("p a (b w) -> p a b w", w=1 << k)
                swap = smask[0:g, :].rearrange("p (b w) -> p b w", w=1 << k)
                swap3 = swap.unsqueeze(1).broadcast_to([g, 3, GE // 2 >> k, 1 << k])
                e.tensor_scalar(swap, first[:, 0], 1 << k, None, ALU.bitwise_and)
                link(e.tensor_copy(kept, first))
                link(e.copy_predicated(first, swap3, second))
                link(e.copy_predicated(second, swap3, kept))
                if k == SORT_STAGES - 1:
                    e.scalar_tensor_tensor(out=rel_f[0:g, ch, :], in0=key_i[0:g, ch, :], scalar=1.0 / GE,
                                           in1=place[0:g, :], op0=ALU.mult, op1=ALU.add).then_inc(s_met, 1)

            def take(n, to_all, ch, g, s_from, s_to):
                e.wait_ge(s_from, n + 1)
                e.tensor_copy(to_all[:, ch * GE:ch * GE + g * GT].rearrange("p (g i) -> p i g", i=GT),
                              mflat.rearrange("p (i g) -> p i g", i=GT)[:, :, 0:g]).then_inc(s_to, 1)

            def take_meta(n):
                if METAS[n][0] == "stats":
                    e.wait_ge(s_mt, n + 1)
                    e.tensor_copy(base_i[:, :], mps[0:1, 0, 0:NG])
                    e.tensor_reduce(flag_f[:, 0:1], mps[0:1, 0, DONE_GROUP:NG], AX, ALU.min)
                    e.tensor_reduce(flag_f[:, 1:2], mps[0:1, 1, 0:NG], AX, ALU.max).then_inc(s_me, 1)
                    e.wait_ge(s_me, n + 1)
                    link(e.tensor_scalar(flag_f[:, 0:1], flag_f[:, 0:1], float(DONE_NODES), None, ALU.is_ge))
                    e.scalar_tensor_tensor(out=flag_i[:, :], in0=flag_f[:, 1:2], scalar=float(WIN - 1), in1=flag_f[:, 0:1],
                                           op0=ALU.is_le, op1=ALU.mult).then_inc(s_flag, 1)
                else:
                    what, ch, g = METAS[n]
                    take(n, {"idx": idx_all, "rel": rel_all, "wgt": wgt_all}[what], ch, g, s_mt, s_me)

            places(0, GA)
            places(1, GB)
            e.wait_ge(s_wgt, 16 * 4)
            for k in range(SORT_STAGES):
                exchange(0, GA, k)
            for k in range(SORT_STAGES):
                exchange(1, GB, k)
                if TAKE_FROM <= k < TAKE_FROM + 4:
                    take_meta(k - TAKE_FROM)
            for n in range(4, len(METAS)):
                take_meta(n)

            def moments(n):
                w = epi_width[n]
                y = acc[:, n * EPI:n * EPI + w]
                e.wait_ge(s_eh, n + 1)
                e.tensor_tensor(y, y, res[:, 2 * n, 0:w], ALU.add).then_inc(s_ey, 1)
                e.wait_ge(s_ey, n + 1)
                if n < NEPI - 1:
                    e.bn_stats(bst[:, n, :], y).then_inc(s_bst, 1)
                else:
                    e.bn_stats(bst[0:F, n, :], y[0:F, :])
                    e.bn_stats(bst[F:P, n, :], y[F:P, 0:w - (P - LAST)]).then_inc(s_bst, 1)

            flag = fast_path_flag(e)
            with e.If(flag < 1):
                e.tensor_scalar(dst_f[0:GA, 0, :], rel_f[0:GA, 0, :], gstat[0:GA, 0, 0:1], None, ALU.add)
                e.tensor_scalar(dst_f[0:GB, 1, :], rel_f[0:GB, 1, :], gstat[0:GB, 1, 0:1], None, ALU.add).then_inc(s_g["dst"], 1)
                take(0, rel_all, 0, GA, s_g["mt"], s_g["me"])
                take(1, rel_all, 1, GB, s_g["mt"], s_g["me"])
                e.memset(acc[:, :], 0.0)
                table_landed(e, NCLS)
                e.memset(zflat[:, 0:2048], 0.0).then_inc(s_g["zero"], 1)
                e.wait_ge(s_g["me"], 2)
                with e.Fori(0, NTILES) as t:
                    e.tensor_copy(gdst[:, 0:1], rel_all[:, bass.ds(t, 1)])
                    e.tensor_copy(gdst[:, 1:2], wgt_all[:, bass.ds(t, 1)]).then_inc(s_g["mul"], 1)
                    e.wait_ge(s_g["mul"], t * 4 + 1)
                    e.tensor_scalar(gdstb[:, :], ones[:, :], gdst[:, 0:1], None, ALU.mult).then_inc(s_g["bcast"], 1)
                    e.wait_ge(s_g["row"], t + 1)
                    e.tensor_scalar(geq[:, :], mps[:, 0, 0:P], gdst[:, 0:1], None, ALU.is_equal).then_inc(s_g["mul"], 1)
                    e.tensor_tensor(gnum[:, 1:2], dumprow[:, :], gdst[:, 0:1], ALU.subtract)
                    e.wait_ge(s_g["mul"], t * 4 + 2)
                    e.scalar_tensor_tensor(out=gjunk[:, :], in0=geq[:, :], scalar=1.0, in1=lower[:, :],
                                           op0=ALU.mult, op1=ALU.mult, accum_out=gnum[:, 0:1]).then_inc(s_g["mul"], 1)
                    e.wait_ge(s_g["mul"], t * 4 + 3)
                    e.tensor_scalar(gnum[:, 2:3], gnum[:, 0:1], 0.0, None, ALU.is_gt).then_inc(s_g["mul"], 1)
                    e.wait_ge(s_g["mul"], t * 4 + 4)
                    e.wait_ge(s_g["idx"], t + 1)
                    e.scalar_tensor_tensor(out=gsidx[:, :], in0=gnum[:, 1:2], scalar=gnum[:, 2:3], in1=gdst[:, 0:1],
                                           op0=ALU.mult, op1=ALU.add)
                    e.wait_ge(s_g["y"], t * 16 + 16)
                    e.tensor_scalar(gyn[:, :], gy[:, :], gdst[:, 1:2], None, ALU.mult).then_inc(s_g["tc"], 1)
                    e.wait_ge(s_g["mm"], t + 1)
                    e.tensor_copy(gsum[:, :], mps[:, 1, 0:F]).then_inc(s_g["sum"], 1)
                for q in range(NQ):
                    e.wait_ge(s_g["tp"], q + 1)
                    e.tensor_copy(acc[0:F, 2 * q * P:(2 * q + 1) * P], aps[0:F, q % 2, 0:P])
                    e.tensor_copy(acc[F:P, (2 * q + 1) * P:(2 * q + 2) * P], aps[F:P, q % 2, 0:P]).then_inc(s_g["back"], 1)
                e.engine_nop().then_inc(s_sum, 1)
                for n in range(EPI_EARLY):
                    moments(n)
            with e.Else():
                def add_up(u):
                    g = units[u][0]
                    base = e.value_load(base_i[0:1, g:g + 1], min_val=0, max_val=N - 1)
                    e.wait_ge(s_agg, unit_end[u] + 1)
                    e.wait_ge(s_acc, u + 1)
                    win = acc[:, bass.ds(base, WIN)]
                    e.tensor_tensor(win, win, aps[:, u % 2, 0:WIN], ALU.add).then_inc(s_acc, 1)

                for t, (col, u, k, size, _) in enumerate(seq):
                    if t >= NOH:
                        e.wait_ge(s_agg, t - NOH + 1)
                    e.tensor_scalar(oh[:, t % NOH, :], iota[:, :], rel_all[:, col:col + 1], wgt_all[:, col:col + 1],
                                    ALU.is_equal, ALU.mult).then_inc(s_oh, 1)
                    if t == 1:
                        e.memset(acc[:, :], 0.0).then_inc(s_acc, 1)
                    if k == size - 1 and u >= 1:
                        add_up(u - 1)
                    if t - NOH - 1 in epi_after:
                        moments(epi_after.index(t - NOH - 1))
                add_up(len(units) - 1)
                e.wait_ge(s_acc, len(units) + 1)
                e.engine_nop().then_inc(s_sum, 1)

            for n in range(EPI_EARLY, NEPI):
                moments(n)
            upper = (NQ - 1) * P + LAST
            for h, nodes, sign in ((0, N - upper, 1.0), (1, upper, -1.0)):
                for to, factor in ((wmean, nodes / N), (wdiff, sign)):
                    for k in range(2):
                        e.tensor_scalar(to[h * F:(h + 1) * F, k * F:(k + 1) * F], stack2[h * F:(h + 1) * F, :], factor, None, ALU.mult)
            e.wait_ge(s_bst, NEPI)
            e.bn_aggr(halves[:, :], bst[:, :, :].rearrange("p a b -> p (a b)")).then_inc(s_st, 1)
            e.wait_ge(s_st, 2)
            link(e.tensor_copy(bmv[:, 0:3], mps[:, 0, 0:3]))
            link(e.tensor_tensor(bmv[:, 9:10], bmv[:, 2:3], bmv[:, 2:3], ALU.mult))
            e.scalar_tensor_tensor(out=bmv[:, 3:4], in0=bmv[:, 9:10], scalar=(N - upper) * upper / N / N,
                                   in1=bmv[:, 1:2], op0=ALU.mult, op1=ALU.add).then_inc(s_st, 1)
            e.wait_ge(s_st, 3)
            e.tensor_scalar(bmv[:, 3:4], bmv[:, 3:4], BN_EPS, None, ALU.add).then_inc(s_st, 1)
            e.wait_ge(s_st, 5)
            e.wait_ge(s_cols, 16 * 8)
            e.reciprocal(bmv[:, 5:6], bmv[:, 4:5]).then_inc(s_st, 1)
            e.wait_ge(s_st, 6)
            e.tensor_tensor(bmv[:, 6:7], bmv[:, 5:6], cols[:, 2:3], ALU.mult).then_inc(s_st, 1)
            e.wait_ge(s_st, 7)
            e.tensor_tensor(bmv[:, 7:8], bmv[:, 0:1], bmv[:, 6:7], ALU.mult).then_inc(s_st, 1)
            e.wait_ge(s_st, 8)
            e.tensor_tensor(bmv[:, 8:9], cols[:, 3:4], bmv[:, 7:8], ALU.subtract).then_inc(s_st, 1)
            e.wait_ge(s_xre, 32)
            for n, w in enumerate(epi_width):
                t0, k = 8 * n, w // P * 2
                e.wait_ge(s_o, n + 1)
                e.tensor_tensor(xo[:, t0:t0 + k, :], xo[:, t0:t0 + k, :],
                                zps[:, n % NZB, 0:k * F].rearrange("p (t f) -> p t f", f=F), ALU.add).then_inc(s_oc, 1)

        @block.tensor
        def _(e):
            e.wait_ge(s_cst, 5)
            e.wait_ge(s_small, 16 * 3)

            def transpose(to, frm, k):
                return e.matmul(to, lhsT=frm, rhs=ident[0:k, 0:k], is_transpose=True, start=True, stop=True)

            def bank(job):
                if at[job] >= NZB:
                    e.wait_ge(*nth[jobs[at[job] - NZB]])
                return bank_of(job)

            transpose(bank(("comp",))[0:R, 0:R], comp_sb[:, :], R).then_inc(s_pz, 1)
            transpose(bank(("resw",))[:, 0:F], resw_sb[:, :], F).then_inc(s_pz, 1)
            e.wait_ge(s_basis, 16)
            e.wait_ge(s_ez, 1)
            for n in range(F // CLS):
                b = bank(("w", n))
                for o in range(CLS):
                    for h in range(2):
                        last = e.matmul(b[h * F:(h + 1) * F, o * R:(o + 1) * R], lhsT=basis_sb[:, :, n * CLS + o],
                                        rhs=compT[:, :], start=True, stop=True)
                last.then_inc(s_pz, 1)

            def transposed_x(c):
                b = bank(("x", c))
                t0, t1 = c * BANK // P, min((c + 1) * BANK // P, NT)
                e.wait_ge(s_dup, c + 1)
                for t in range(t0, t1):
                    last = transpose(b[:, (t - t0) * P:(t - t0 + 1) * P],
                                     xdup[:, c % 2, t - t0, :, :].rearrange("p a f -> p (a f)"), P)
                last.then_inc(s_pz, 1)

            def three_parts(to, stationary, moving):
                for a, (px, pw) in enumerate(((0, 0), (0, 1), (1, 2))):
                    last = e.matmul(to, lhsT=stationary(px, pw), rhs=moving(px, pw), start=(a == 0), stop=(a == 2))
                return last

            def product(c, t):
                b = bank(("z", c, t))
                ch, n0 = divmod(t * P, BANK)
                if c == 0 and n0 == 0:
                    e.wait_ge(s_xo, ch + 1)
                    e.wait_ge(s_p2, X0 + ch + 1)
                three_parts(b, lambda px, pw: xp[:, ch, px, n0:n0 + P],
                            lambda px, pw: wp[:, pw, c * CLS:(c + 1) * CLS, :].rearrange("p r f -> p (r f)")).then_inc(s_pz, 1)

            for c in range(NCH + AHEAD):
                if c < NCH:
                    transposed_x(c)
                if c >= AHEAD:
                    for t in range((c - AHEAD) * 4, min((c - AHEAD + 1) * 4, NT)):
                        product(0, t)

            def edges(ch, g, frm, s_to):
                for i in range(GT):
                    last = transpose(mflat[:, i * P:i * P + g], frm[0:g, ch, i * P:(i + 1) * P], g)
                last.then_inc(s_to, 1)

            late_jobs = [("z", c, t) for c in range(FIRST_CLS, NCLS) for t in range(NT)] + [("r", n) for n in range(NEPI)]

            def late_job(kind, c, *t):
                if kind == "z":
                    product(c, *t)
                    return
                b = bank(("r", c))
                for ch in range(2 * c, min(2 * c + 2, NCH)):
                    tiles = min(BANK, NT * P - ch * BANK) // P
                    for h in range(2):
                        last = three_parts(
                            b[h * F:(h + 1) * F, (ch - 2 * c) * 2 * P:(ch - 2 * c) * 2 * P + tiles // 2 * P],
                            lambda px, pw: wp[:, pw, R, :],
                            lambda px, pw: xp[:, ch, px, 0:tiles * P].rearrange("p (t a n) -> p t a n", a=2, n=P)[:, :, h, :])
                last.then_inc(s_pz, 1)

            def meta(n):
                if n:
                    e.wait_ge(s_me, n)
                if METAS[n][0] == "stats":
                    for k, b in ((0, 0), (2, 1)):
                        transpose(mps[0:1, b, 0:GA], gstat[:, 0, k:k + 1], GA)
                        last = transpose(mps[0:1, b, GA:NG], gstat[0:GB, 1, k:k + 1], GB)
                    last.then_inc(s_mt, 1)
                else:
                    what, ch, g = METAS[n]
                    e.wait_ge(s_met, ch + 1)
                    edges(ch, g, {"idx": idx_f, "rel": rel_f, "wgt": wgt_f}[what], s_mt)

            for c in range(1, FIRST_CLS):
                for t in range(NT):
                    if (c, t) in METAS_AT:
                        meta(METAS_AT.index((c, t)))
                    product(c, t)

            def sum_halves(n):
                if n == 0:
                    e.wait_ge(s_ez, emptied[s_ez])
                if n >= NZB:
                    e.wait_ge(s_eh, n - NZB + 1)
                w = epi_width[n]
                sums = acc[:, n * EPI:n * EPI + 2 * w].rearrange("p (t a n) -> p t a n", a=2, n=P)
                for h in range(2):
                    last = e.matmul(zps[h * F:(h + 1) * F, n % NZB, 0:w], lhsT=stack2[:, :], rhs=sums[:, :, h, :],
                                    start=True, stop=True)
                last.then_inc(s_e1, 1)

            flag = fast_path_flag(e)
            with e.If(flag < 1):
                for job in late_jobs:
                    late_job(*job)
                e.wait_ge(s_g["dst"], 1)
                edges(0, GA, dst_f, s_g["mt"])
                e.wait_ge(s_g["me"], 1)
                edges(1, GB, dst_f, s_g["mt"])
                e.wait_ge(s_g["me"], 2)
                with e.Fori(0, NTILES) as t:
                    e.wait_ge(s_g["bcast"], t + 1)
                    transpose(mps[:, 0, 0:P], gdstb[:, :], P).then_inc(s_g["row"], 1)
                    e.wait_ge(s_g["tc"], t + 1)
                    e.matmul(mps[:, 1, 0:F], lhsT=geq[:, :], rhs=gyn[:, :], start=True, stop=True).then_inc(s_g["mm"], 1)
                e.wait_ge(s_g["back"], 16)
                for q in range(NQ):
                    if q >= 2:
                        e.wait_ge(s_g["back"], 16 + q - 1)
                    transpose(aps[:, q % 2, 0:P], xo[:, 2 * q:2 * q + 2, :].rearrange("p t f -> p (t f)"), P).then_inc(s_g["tp"], 1)
                e.wait_ge(s_sum, 1)
                for n in range(EPI_EARLY):
                    sum_halves(n)
            with e.Else():
                def sum_tile(t):
                    _, u, k, size, _ = seq[t]
                    if k == 0 and u >= 2:
                        e.wait_ge(s_acc, u)
                    e.wait_ge(s_y[t % NY], 16 * (t // NY + 1))
                    e.wait_ge(s_oh, t + 1)
                    h = (k % 2) * F
                    e.matmul(aps[h:h + F, u % 2, 0:WIN], lhsT=ys[:, t % NY, :], rhs=oh[:, t % NOH, :],
                             start=(k < 2), stop=(k >= size - 2)).then_inc(s_agg, 1)

                clock, t, gathered = 0.0, 0, LANDING_US
                for job in late_jobs:
                    done = job[1] if job[0] == "z" else NCLS
                    if job[0] == "z" and job[2] == 0:
                        gathered = max(gathered, clock + LANDING_US) if seq[t][4] >= done else gathered
                    while seq[t][4] <= min(done, NCLS - 1) and clock >= gathered:
                        sum_tile(t)
                        t += 1
                        clock += SUM_US
                        gathered += GATHER_US
                    late_job(*job)
                    clock += PRODUCT_US
                for t in range(t, NTILES):
                    sum_tile(t)
                    if t in epi_after:
                        if t == epi_after[0]:
                            e.wait_ge(s_acc, done_unit + 2)
                        sum_halves(epi_after.index(t))

            e.wait_ge(s_sum, 1)
            for n in range(EPI_EARLY, NEPI):
                sum_halves(n)
            e.wait_ge(s_st, 1)
            e.matmul(mps[:, 0, 0:2], lhsT=wmean[:, :], rhs=halves[:, :], start=True, stop=True)
            e.matmul(mps[:, 0, 2:3], lhsT=wdiff[:, :], rhs=halves[:, 0:1], start=True, stop=True).then_inc(s_st, 1)
            for n, w in enumerate(epi_width):
                e.wait_ge(s_sc, n + 1)
                if n >= NZB:
                    e.wait_ge(s_oc, n - NZB + 1)
                for q in range(w // P):
                    last = transpose(zps[:, n % NZB, q * P:(q + 1) * P], acc[:, n * EPI + q * P:n * EPI + (q + 1) * P], P)
                last.then_inc(s_o, 1)


_INS = ["x", "src", "dst", "edge_type_64", "edge_weight1", "L0_gnn_basis", "L0_gnn_comp", "L0_gnn_bias",
        "L0_gnn_res_w", "L0_gnn_res_b", "L0_gnn_gamma", "L0_gnn_beta"]


def kernel(**inputs):
    import numpy as np
    import concourse.bacc as bacc
    from concourse.bass_utils import run_bass_kernel_spmd

    nc = bacc.Bacc("TRN2", target_bir_lowering=False, num_devices=1)
    arrays, args = {}, []
    for name in _INS:
        a = np.ascontiguousarray(inputs[name])
        if name == "edge_weight1":
            a = a.reshape(-1)
        arrays[f"in_{name}"] = a
        args.append(nc.dram_tensor(f"in_{name}", a.shape, mybir.dt.from_np(a.dtype), kind="ExternalInput").ap())
    shape = inputs["x"].shape
    args.append(nc.dram_tensor("out_x", shape, F32, kind="ExternalOutput").ap())
    rgcn_kernel(nc, *args)
    r = run_bass_kernel_spmd(nc, [arrays], core_ids=[0])
    return r.results[0]["out_x"]
```
